# Optimizing a Trainium2 kernel written in Bass

```python
import numpy as np
import jax
import jax.numpy as jnp

def _softmax(x, axis=-1):
    return jax.nn.softmax(x, axis=axis)

def _gelu(x):
    return jax.nn.gelu(x, approximate=True)

def _silu(x):
    return jax.nn.silu(x)

def _sigmoid(x):
    return jax.nn.sigmoid(x)

def _layernorm(x, axis=-1, eps=1e-05):
    m = jnp.mean(x, axis=axis, keepdims=True)
    v = jnp.var(x, axis=axis, keepdims=True)
    return (x - m) / jnp.sqrt(v + eps)

def _scatter_add(tgt, idx, src, axis=0):
    return tgt.at[idx].add(src)

def _segment_sum(src, seg, n):
    return jax.ops.segment_sum(src, seg, n)
kernel_name = 'mk_gnn_preln_d2_gnn_r64_537125'

def setup_inputs(seed: int=0):
    np.random.seed(seed)
    _w = jnp.asarray

    def _rec_inputs():
        import jax
        import jax.numpy as jnp
        _gk = jax.random.key(seed)
        x = -0.0001006 + 1 * jax.random.normal(jax.random.fold_in(_gk, 1), (100000, 48), jnp.float32)
        src = jax.random.randint(jax.random.fold_in(_gk, 2), (25000,), 0, 100000, jnp.int32)
        dst = jax.random.randint(jax.random.fold_in(_gk, 3), (25000,), 0, 100000, jnp.int32)
        _o = jnp.argsort(dst, stable=True)
        src = src[_o]
        dst = dst[_o]
        edge_attr_40 = jax.random.uniform(jax.random.fold_in(_gk, 12), (25000, 40), jnp.float32, 0.0, 1)
        edge_weight = jax.random.uniform(jax.random.fold_in(_gk, 14), (25000,), jnp.float32, 0.0, 0.999999)
        node_type_119 = jax.random.randint(jax.random.fold_in(_gk, 15), (100000,), 0, 119, jnp.int32)
        node_vec = jax.random.uniform(jax.random.fold_in(_gk, 16), (100000,), jnp.float32, 0.0, 1.49999)
        return (x, src, dst, edge_attr_40, edge_weight, node_type_119, node_vec)
    x, src, dst, edge_attr_40, edge_weight, node_type_119, node_vec = _rec_inputs()

    def _L0_gnn_setup():
        import jax, jax.numpy as jnp
        import numpy as np
        NUM_NODES = 100000
        key = jax.random.key(seed)
        k1, k2, k3 = jax.random.split(key, 3)
        x = jax.random.normal(k1, (NUM_NODES, 48), dtype=jnp.float32)
        edge_index = jax.random.randint(k2, (2, 25000), 0, NUM_NODES, dtype=jnp.int64)
        edge_weight = jax.random.uniform(k3, (25000,), dtype=jnp.float32)
        return {'x': x, 'edge_index': edge_index, 'edge_weight': edge_weight}
    _L0_gnn_all = _L0_gnn_setup()
    _L0_gnn_in = {k: v for k, v in _L0_gnn_all.items() if k in ()}
    del _L0_gnn_all

    def _L1_gnn_setup():
        import jax, jax.numpy as jnp
        import numpy as np
        CUTOFF = 6.0
        LN_EPS = 1e-05
        key = jax.random.key(seed)
        ks = jax.random.split(key, 16)
        N, E, H, R, NEL, G = (50000, 12500, 48, 40, 119, 32)
        inp = {'h': jax.random.normal(ks[0], (N, H), jnp.float32), 'edge_index': jax.random.randint(ks[1], (2, E), 0, N, jnp.int64), 'edge_attr': jax.random.uniform(ks[2], (E, R), jnp.float32), 'distances': jax.random.uniform(ks[3], (E,), jnp.float32) * 7.0, 'atom_z': jax.random.randint(ks[4], (N,), 0, NEL, jnp.int64), 'node_mult': jax.random.uniform(ks[5], (N,), jnp.float32) + 0.5, 'batch': jnp.zeros((N,), jnp.int64), 'W1': jax.random.normal(ks[6], (H, R), jnp.float32) / np.sqrt(R), 'b1': jax.random.normal(ks[7], (H,), jnp.float32) * 0.01, 'W2': jax.random.normal(ks[8], (H, H), jnp.float32) / np.sqrt(H), 'b2': jax.random.normal(ks[9], (H,), jnp.float32) * 0.01, 'emb': jax.random.normal(ks[10], (NEL, G), jnp.float32) * 0.01, 'adaptW': jax.random.normal(ks[11], (G, G), jnp.float32) * 0.01, 'gamma': jnp.ones((H,), jnp.float32), 'beta': jnp.zeros((H,), jnp.float32)}
        return inp
    _L1_gnn_all = _L1_gnn_setup()
    _L1_gnn_in = {k: v for k, v in _L1_gnn_all.items() if k in ('W1', 'b1', 'W2', 'b2', 'emb', 'adaptW', 'gamma', 'beta')}
    del _L1_gnn_all
    return {'x': x, 'src': src, 'dst': dst, 'edge_attr_40': edge_attr_40, 'edge_weight': edge_weight, 'node_type_119': node_type_119, 'node_vec': node_vec, 'L1_gnn_W1': _L1_gnn_in['W1'], 'L1_gnn_b1': _L1_gnn_in['b1'], 'L1_gnn_W2': _L1_gnn_in['W2'], 'L1_gnn_b2': _L1_gnn_in['b2'], 'L1_gnn_emb': _L1_gnn_in['emb'], 'L1_gnn_adaptW': _L1_gnn_in['adaptW'], 'L1_gnn_gamma': _L1_gnn_in['gamma'], 'L1_gnn_beta': _L1_gnn_in['beta']}

def reference(x, src, dst, edge_attr_40, edge_weight, node_type_119, node_vec, L1_gnn_W1, L1_gnn_b1, L1_gnn_W2, L1_gnn_b2, L1_gnn_emb, L1_gnn_adaptW, L1_gnn_gamma, L1_gnn_beta):
    import jax
    import jax.numpy as jnp

    def _L0_gnn_ref(x, edge_index, edge_weight):
        import jax, jax.numpy as jnp
        import numpy as np
        NUM_NODES = 100000
        src, dst = (edge_index[0], edge_index[1])
        msgs = x[src] * edge_weight[:, None]
        out = jax.ops.segment_sum(msgs, dst, num_segments=NUM_NODES)
        return out

    def _L1_gnn_ref(h, edge_index, edge_attr, distances, atom_z, node_mult, batch, W1, b1, W2, b2, emb, adaptW, gamma, beta):
        import jax, jax.numpy as jnp
        import numpy as np
        CUTOFF = 6.0
        LN_EPS = 1e-05
        src, dst = (edge_index[0], edge_index[1])
        N = h.shape[0]
        gate = jax.nn.silu(edge_attr @ W1.T + b1) @ W2.T + b2
        ei = emb[atom_z[src]]
        ej = emb[atom_z[dst]]
        adapt_logit = jnp.sum(ei * (ej @ adaptW.T), axis=-1, keepdims=True)
        gate = gate + adapt_logit
        cw = jnp.where(distances < CUTOFF, 0.5 * (jnp.cos(jnp.pi * distances / CUTOFF) + 1.0), 0.0)
        mj = node_mult[dst]
        msg = gate * h[dst] * (cw * mj)[:, None]
        agg = jax.ops.segment_sum(msg, src, num_segments=N)
        tot = jax.ops.segment_sum(mj, src, num_segments=N)
        agg = agg / jnp.clip(tot, 1e-08, None)[:, None]
        x = h + agg
        mu = jnp.mean(x, axis=-1, keepdims=True)
        var = jnp.mean(jnp.square(x - mu), axis=-1, keepdims=True)
        return (x - mu) / jnp.sqrt(var + LN_EPS) * gamma + beta
    edge_index = jnp.stack([src, dst])
    batch0 = jnp.zeros((100000,), jnp.int32)
    h = jnp.maximum(_layernorm(x, axis=-1), 0.0)
    x = x + _L0_gnn_ref(h, edge_index, edge_weight)
    h = jnp.maximum(_layernorm(x, axis=-1), 0.0)
    x = x + _L1_gnn_ref(h, edge_index, edge_attr_40, edge_weight, node_type_119, node_vec, batch0, L1_gnn_W1, L1_gnn_b1, L1_gnn_W2, L1_gnn_b2, L1_gnn_emb, L1_gnn_adaptW, L1_gnn_gamma, L1_gnn_beta)
    return x

_drawn_inputs = setup_inputs


def setup_inputs(seed=0):
    import zlib

    import numpy as np

    out = dict(_drawn_inputs(seed))
    spreads = {'L1_gnn_gamma': (1.0, 0.2), 'L1_gnn_beta': (0.0, 0.1)}
    factors = {'node_vec': 46.833,
     'L1_gnn_b1': 34.148,
     'L1_gnn_b2': 21.497,
     'L1_gnn_emb': 64.0,
     'L1_gnn_adaptW': 64.0}
    for name, (base, spread) in spreads.items():
        noise = np.random.default_rng([zlib.crc32(name.encode()), seed]).standard_normal(out[name].shape)
        drawn = base * np.exp(spread * noise) if base else spread * noise
        out[name] = jnp.asarray(drawn.astype(out[name].dtype))
    for name, factor in factors.items():
        out[name] = (out[name] * factor).astype(out[name].dtype)
    return out
```

```python
import concourse.bass as bass
from concourse import mybir
from contextlib import ExitStack


class Turn:

    def __init__(self, base, ring, k=None):
        self.base, self.ring, self.k = base, ring, k

    @property
    def number(self):
        return self.base if self.k is None else self.base + self.ring * self.k

    @property
    def slot(self):
        return self.base % self.ring

    @property
    def uses(self):
        return self.base // self.ring if self.k is None else self.base // self.ring + self.k

    def ahead(self, turns):
        return Turn(self.base + turns, self.ring, self.k)

    @property
    def slot_is_new(self):
        return self.k is None and self.base < self.ring


def turns(eng, count, ring, body, lead, tail=0):
    rounds, rest = divmod(count - lead - tail, ring)
    assert rest == 0 and lead >= ring
    for n in range(lead):
        body(Turn(n, ring))
    with eng.Fori(0, rounds) as k:
        for r in range(ring):
            body(Turn(lead + r, ring, k))
    for n in range(count - tail, count):
        body(Turn(n, ring))


class Steps:

    def __init__(self, eng, sem, first):
        self.eng, self.sem, self.first, self.n = eng, sem, first, 0

    def add(self, instruction):
        instruction.then_inc(self.sem, 1)
        self.n += 1

    def wait(self):
        self.eng.wait_ge(self.sem, self.first + self.n)


def gnn_kernel(nc, x, src, dst, edge_attr, edge_weight, node_type, node_vec, W1, b1, W2, b2, emb, adaptW, gamma,
               beta, out):
    fp32 = mybir.dt.float32
    i32 = mybir.dt.int32
    ALU = mybir.AluOpType
    ACT = mybir.ActivationFunctionType
    AX = mybir.AxisListType

    P = 128
    N, H = x.shape
    E, R = edge_attr.shape
    KINDS, DIM = emb.shape
    EPS = 1e-5
    CUTOFF = 6.0
    ROUND = 1.5 * 2.0 ** 23

    FULL = E // P
    REM = E - P * FULL
    TILES = FULL + 1
    U = 4
    GROUPS = TILES // U
    assert GROUPS * U == TILES
    RING = 2
    W = H + 2
    TRASH = N
    ROWS = N + U * P
    SPAN = [(U - j) * P for j in range(U)]
    SPAN_AT = [sum(SPAN[:j]) for j in range(U)]

    NR = 16
    CHUNK = P * NR
    FULL_CHUNKS = N // CHUNK
    LAST_P = (N - FULL_CHUNKS * CHUNK) // NR
    CHUNKS = FULL_CHUNKS + 1
    assert FULL_CHUNKS * CHUNK + LAST_P * NR == N
    TRING = 3

    table = nc.dram_tensor("node_table", (ROWS, W), fp32, kind="Internal").ap()
    sums = nc.dram_tensor("edge_sums", (ROWS, W), fp32, kind="Internal").ap()

    def chunk(t, c):
        if isinstance(c, int) and c == FULL_CHUNKS:
            return t[FULL_CHUNKS * CHUNK:N].rearrange("(p r) f -> p (r f)", r=NR)
        v = t[0:FULL_CHUNKS * CHUNK].rearrange("(c p r) f -> c p (r f)", p=P, r=NR)
        return v[bass.ds(c, 1)].rearrange("a p f -> (a p) f")

    def parts(c):
        return LAST_P if isinstance(c, int) and c == FULL_CHUNKS else P

    ctx = ExitStack()
    with ctx:
        def sb(name, shape, dt=fp32):
            return ctx.enter_context(nc.sbuf_tensor(name, shape, dt))

        def sem(name):
            return ctx.enter_context(nc.semaphore(name))

        order = sb("order", [P, 3 * TILES], i32)
        keys_i = sb("keys_i", [P, 2, TILES], i32)
        keys = sb("keys", [P, 2, TILES])
        rel = sb("rel", [P, 2, GROUPS, U])
        trash_i = sb("trash_i", [P, U], i32)
        trash = sb("trash", [P, U])
        ew = sb("ew", [P, TILES])
        cutoff_w = sb("cutoff_w", [P, TILES])
        cw_t = sb("cw_t", [P, TILES])
        half_pi = sb("half_pi", [P, 1])
        dev0 = sb("dev0", [P, TILES, H])
        gate = sb("gate", [P, TILES, H])
        var0 = sb("var0", [P, TILES])
        rw = sb("rw", [P, TILES])
        type_src = sb("type_src", [P, TILES])
        ident = sb("ident", [P, P])
        upto = sb("upto", [P, U * P])
        kind_row = sb("kind_row", [P, KINDS])
        kind_col = sb("kind_col", [P, 1])
        zeros = sb("zeros", [P, NR * W])
        gamma_b = sb("gamma_b", [P, H])
        beta_b = sb("beta_b", [P, H])
        w1_in = sb("w1_in", [H, R])
        w2_in = sb("w2_in", [H, H])
        emb_in = sb("emb_in", [KINDS, DIM])
        adapt_in = sb("adapt_in", [DIM, DIM])
        w1T = sb("w1T", [R + 1, H])
        w2T = sb("w2T", [H + 1, H])
        embT = sb("embT", [DIM, KINDS])
        adapted = sb("adapted", [DIM, KINDS])
        logits = sb("logits", [KINDS, KINDS])
        vec_in = sb("vec_in", [P, CHUNKS, NR])
        type_in = sb("type_in", [P, CHUNKS, NR], i32)
        x_in = sb("x_in", [P, RING, NR, H])
        rows_out = sb("rows_out", [P, RING, NR, W])
        slot_idx = sb("slot_idx", [P, RING, U], i32)
        got = sb("got", [P, RING, U, W])
        got_x = sb("got_x", [P, RING, U, H])
        got_type = sb("got_type", [P, RING, U], i32)
        s4 = sb("s4", [P, U])
        m4 = sb("m4", [P, U])
        v4 = sb("v4", [P, U])
        sq4 = sb("sq4", [P, U, H])
        dev = sb("dev", [P, RING, U, H])
        sd4 = sb("sd4", [P, RING, U])
        ve4 = sb("ve4", [P, RING, U])
        lg4 = sb("lg4", [P, U])
        cf4 = sb("cf4", [P, U])
        gl4 = sb("gl4", [P, U, H])
        hit = sb("hit", [P, U, KINDS])
        key4 = sb("key4", [P, RING, U])
        type4 = sb("type4", [P, U])
        onehot = sb("onehot", [KINDS, U * P])
        msg = sb("msg", [P, RING, U, W])
        same = sb("same", [P, RING, sum(SPAN)])
        count = sb("count", [P, RING, U])
        last4 = sb("last4", [P, U])
        off4 = sb("off4", [P, U])
        put_idx = sb("put_idx", [P, RING, U], i32)
        put = sb("put", [P, RING, U, W])
        attr_in = sb("attr_in", [P, RING, U, R])
        attrT = sb("attrT", [64, U * P])
        sig = sb("sig", [H, U * P])
        hidden = sb("hidden", [64, U * P])
        t_x = sb("t_x", [P, TRING, NR, W])
        t_s = sb("t_s", [P, TRING, NR, W])
        t_d = sb("t_d", [P, TRING, NR, H])
        t_y = sb("t_y", [P, TRING, NR, H])
        t_q1 = sb("t_q1", [P, TRING, NR, H])
        t_q2 = sb("t_q2", [P, TRING, NR, H])
        t_m = sb("t_m", [P, NR])
        t_inv = sb("t_inv", [P, TRING, NR])
        t_v1 = sb("t_v1", [P, TRING, NR])
        t_v2 = sb("t_v2", [P, TRING, NR])
        t_sd1 = sb("t_sd1", [P, TRING, NR])
        t_sd2 = sb("t_sd2", [P, TRING, NR])

        bank = [ctx.enter_context(nc.psum_tensor(f"bank{i}", [P, 512], fp32)) for i in range(8)]
        ps_key = bank[0:2]
        ps_sum = bank[2:4]
        ps_attr, ps_hid, ps_gate = bank[4:7]
        ps_type, ps_logit = bank[4:6]

        keys_loaded = sem("keys_loaded")
        order_loaded = sem("order_loaded")
        ew_loaded = sem("ew_loaded")
        nodes_loaded = sem("nodes_loaded")
        weights_loaded = sem("weights_loaded")
        pads_set = sem("pads_set")
        const_set = sem("const_set")
        w_turned = sem("w_turned")
        w_copied = sem("w_copied")
        cw_angle = sem("cw_angle")
        cw_sin = sem("cw_sin")
        setup_step = sem("setup_step")
        setup_done = sem("setup_done")
        x_loaded = [sem(f"x_loaded{i}") for i in range(RING)]
        rows_built = sem("rows_built")
        rows_stored = [sem(f"rows_stored{i}") for i in range(RING)]
        act_step = sem("act_step")
        trash_zeroed = sem("trash_zeroed")
        sums_zeroed = sem("sums_zeroed")
        idx_ready = sem("idx_ready")
        gathered = [sem(f"gathered{i}") for i in range(RING)]
        a_step = sem("a_step")
        var0_ready = sem("var0_ready")
        sd0_ready = sem("sd0_ready")
        b_step = sem("b_step")
        c_step = sem("c_step")
        key4_ready = sem("key4_ready")
        keys_turned = sem("keys_turned")
        same_ready = sem("same_ready")
        put_idx_ready = sem("put_idx_ready")
        summed = sem("summed")
        put_ready = sem("put_ready")
        added = [sem(f"added{i}") for i in range(RING)]
        drained = sem("drained")
        attr_loaded = [sem(f"attr_loaded{i}") for i in range(RING)]
        attr_turned = sem("attr_turned")
        attrT_ready = sem("attrT_ready")
        hid_done = sem("hid_done")
        sig_ready = sem("sig_ready")
        hidden_ready = sem("hidden_ready")
        gate_done = sem("gate_done")
        gate_copied = sem("gate_copied")
        var_ready = sem("var_ready")
        sd_ready = sem("sd_ready")
        type4_ready = sem("type4_ready")
        types_turned = sem("types_turned")
        onehot_ready = sem("onehot_ready")
        logit_done = sem("logit_done")
        all_added = sem("all_added")
        passed = sem("passed")
        t_loaded = [sem(f"t_loaded{i}") for i in range(TRING)]
        t_step = sem("t_step")
        t_dev = sem("t_dev")
        t_inv_ready = sem("t_inv_ready")
        t_agg = sem("t_agg")
        t_sq1 = sem("t_sq1")
        t_var1 = sem("t_var1")
        t_std1 = sem("t_std1")
        t_dev2 = sem("t_dev2")
        t_sq2 = sem("t_sq2")
        t_var2 = sem("t_var2")
        t_std2 = sem("t_std2")
        t_norm = sem("t_norm")
        t_pstep = sem("t_pstep")
        t_out = sem("t_out")
        t_stored = [sem(f"t_stored{i}") for i in range(TRING)]

        block = ctx.enter_context(nc.Block())

        def hold(eng):
            eng.sem_inc(passed, 1)

        def wide(ap, n):
            return ap.unsqueeze(2).broadcast_to([ap.shape[0], ap.shape[1], n])

        def rows(ap, k):
            return ap.unsqueeze(1).broadcast_to([ap.shape[0], k, ap.shape[1]])

        def group(ap, g):
            return ap[:, bass.ds(U * g, U)]

        LEAD_E = 3
        B_AT = GROUPS
        C_AT = 2 * GROUPS
        C_STEPS = 14

        @block.sync
        def _(sp):
            def by_edge(a):
                return a[0:P * FULL].rearrange("(p t) -> p t", p=P)

            def rest(a):
                return a[P * FULL:E].rearrange("(p t) -> p t", t=1)

            sp.wait_ge(pads_set, 3)
            for n, a in enumerate((src, src, dst)):
                sp.dma_start(order[:, n * TILES:n * TILES + FULL], by_edge(a)).then_inc(order_loaded, 16)
                sp.dma_start(order[0:REM, n * TILES + FULL:(n + 1) * TILES], rest(a)).then_inc(order_loaded, 16)
            for n, a in enumerate((dst, src)):
                sp.dma_start(keys_i[:, n, 0:FULL], by_edge(a)).then_inc(keys_loaded, 16)
                sp.dma_start(keys_i[0:REM, n, FULL:TILES], rest(a)).then_inc(keys_loaded, 16)
            sp.dma_start(ew[:, 0:FULL], by_edge(edge_weight)).then_inc(ew_loaded, 16)
            sp.dma_start(ew[0:REM, FULL:TILES], rest(edge_weight)).then_inc(ew_loaded, 16)
            for t, a in ((vec_in, node_vec), (type_in, node_type)):
                sp.dma_start(t[:, 0:FULL_CHUNKS, :], a[0:FULL_CHUNKS * CHUNK].rearrange("(c p r) -> p c r", p=P, r=NR))\
                    .then_inc(nodes_loaded, 16)
                sp.dma_start(t[0:LAST_P, FULL_CHUNKS, :], a[FULL_CHUNKS * CHUNK:N].rearrange("(p r) -> p r", r=NR))\
                    .then_inc(nodes_loaded, 16)

            def load_x(t):
                sp.dma_start(x_in[0:parts(t.number), t.slot].rearrange("p r f -> p (r f)"), chunk(x, t.number))\
                    .then_inc(x_loaded[t.slot], 16)

            def store_rows(t):
                sp.wait_ge(rows_built, t.number + 1)
                sp.dma_start(chunk(table, t.number), rows_out[0:parts(t.number), t.slot].rearrange("p r f -> p (r f)"))\
                    .then_inc(rows_stored[t.slot], 16)

            load_x(Turn(0, RING))
            load_x(Turn(1, RING))
            for a, w in ((w1_in, W1), (w2_in, W2), (emb_in, emb), (adapt_in, adaptW)):
                sp.dma_start(a[:, :], w[:, :]).then_inc(weights_loaded, 16)
            sp.dma_start(w1T[R:R + 1, :], b1.rearrange("(a h) -> a h", a=1)).then_inc(weights_loaded, 16)
            sp.dma_start(w2T[H:H + 1, :], b2.rearrange("(a h) -> a h", a=1)).then_inc(weights_loaded, 16)
            sp.dma_start(gamma_b[:, :], gamma.rearrange("(a h) -> a h", a=1).broadcast_to([P, H])).then_inc(weights_loaded, 16)
            sp.dma_start(beta_b[:, :], beta.rearrange("(a h) -> a h", a=1).broadcast_to([P, H])).then_inc(weights_loaded, 16)

            def table_turn(t):
                store_rows(t)
                if not (isinstance(t.number, int) and t.number + RING >= CHUNKS):
                    load_x(t.ahead(RING))

            turns(sp, CHUNKS, RING, table_turn, lead=3, tail=4)

            sp.wait_ge(const_set, 4)
            sp.dma_start(table[N:ROWS].rearrange("(p r) f -> p (r f)", p=P), zeros[:, 0:U * W]).then_inc(trash_zeroed, 16)
            sp.dma_start(sums[N:ROWS].rearrange("(p r) f -> p (r f)", p=P), zeros[:, 0:U * W]).then_inc(sums_zeroed, 16)
            sp.dma_start(chunk(sums, FULL_CHUNKS), zeros[0:LAST_P, :]).then_inc(sums_zeroed, 16)
            with sp.Fori(0, FULL_CHUNKS) as c:
                sp.dma_start(chunk(sums, c), zeros[:, :]).then_inc(sums_zeroed, 16)

            def load_attr(t):
                if not t.slot_is_new:
                    sp.wait_ge(attr_turned, t.number - 1)
                if isinstance(t.number, int) and t.number == GROUPS - 1:
                    at = U * t.number
                    sp.dma_start(attr_in[:, t.slot, 0:U - 1, :],
                                 edge_attr[0:P * FULL].rearrange("(p t) r -> p t r", p=P)[:, at:at + U - 1, :])\
                        .then_inc(attr_loaded[t.slot], 16)
                    sp.dma_start(attr_in[0:REM, t.slot, U - 1, :], edge_attr[P * FULL:E]).then_inc(attr_loaded[t.slot], 16)
                else:
                    sp.dma_start(attr_in[:, t.slot, :, :],
                                 edge_attr[0:P * FULL].rearrange("(p t) r -> p t r", p=P)[:, bass.ds(U * t.number, U), :])\
                        .then_inc(attr_loaded[t.slot], 16)

            turns(sp, GROUPS, RING, load_attr, lead=2, tail=1)

            sp.wait_ge(all_added, 1)

            def load_chunk(t):
                n = parts(t.number)
                sp.dma_start(t_x[0:n, t.slot].rearrange("p r f -> p (r f)"), chunk(table, t.number))\
                    .then_inc(t_loaded[t.slot], 16)
                sp.dma_start(t_s[0:n, t.slot].rearrange("p r f -> p (r f)"), chunk(sums, t.number))\
                    .then_inc(t_loaded[t.slot], 16)

            for n in range(TRING):
                load_chunk(Turn(n, TRING))

            def last_turn(t):
                n = parts(t.number)
                sp.wait_ge(t_out, t.number + 1)
                sp.dma_start(chunk(out, t.number), t_y[0:n, t.slot].rearrange("p r f -> p (r f)"))\
                    .then_inc(t_stored[t.slot], 16)
                if not (isinstance(t.number, int) and t.number + TRING >= CHUNKS):
                    load_chunk(t.ahead(TRING))

            turns(sp, CHUNKS, TRING, last_turn, lead=3, tail=4)
            for n in range(CHUNKS - TRING, CHUNKS):
                t = Turn(n, TRING)
                sp.wait_ge(t_stored[t.slot], 16 * (t.uses + 1))

        @block.gpsimd
        def _(gp):
            for n in range(2):
                last = gp.memset(order[:, (n + 1) * TILES - 1:(n + 1) * TILES], 0)
            last.then_inc(pads_set, 1)
            for n in range(2):
                last = gp.iota(keys_i[:, n, FULL:TILES], pattern=[[0, 1]], base=TRASH + (U - 1) * P, channel_multiplier=1)
            gp.iota(order[:, 3 * TILES - 1:3 * TILES], pattern=[[0, 1]], base=TRASH + (U - 1) * P,
                    channel_multiplier=1).then_inc(pads_set, 1)
            gp.iota(trash_i[:, :], pattern=[[P, U]], base=TRASH, channel_multiplier=1).then_inc(const_set, 1)
            gp.iota(kind_row[:, :], pattern=[[1, KINDS]], base=0, channel_multiplier=0,
                    allow_small_or_imprecise_dtypes=True).then_inc(const_set, 1)
            gp.iota(kind_col[:, :], pattern=[[0, 1]], base=0, channel_multiplier=1,
                    allow_small_or_imprecise_dtypes=True).then_inc(const_set, 1)
            gp.memset(zeros[:, :], 0.0).then_inc(const_set, 1)
            gp.memset(ident[:, :], 0.0).then_inc(const_set, 1)
            gp.memset(upto[:, :], 1.0).then_inc(const_set, 1)
            gp.wait_ge(const_set, 6)
            gp.affine_select(out=ident[:, :], in_=ident[:, :], compare_op=ALU.not_equal, fill=1.0, base=0,
                             pattern=[[-1, P]], channel_multiplier=1).then_inc(const_set, 1)
            gp.affine_select(out=upto[:, 0:P], in_=upto[:, 0:P], compare_op=ALU.is_ge, fill=0.0, base=0,
                             pattern=[[1, P]], channel_multiplier=-1).then_inc(const_set, 1)

            def gather(t, source, dest):
                gp.wait_ge(idx_ready, t.number + 1)
                hold(gp)
                for u in range(U):
                    gp.indirect_dma_start(out=dest[:, t.slot, u], out_offset=None, in_=source,
                                          in_offset=bass.IndirectOffsetOnAxis(ap=slot_idx[:, t.slot, u:u + 1], axis=0))\
                        .then_inc(gathered[t.slot], 16)

            def add(t, dest):
                gp.wait_ge(put_idx_ready, t.number + 1)
                gp.wait_ge(put_ready, t.number + 1)
                hold(gp)
                for u in range(U):
                    gp.indirect_dma_start(out=dest, out_offset=bass.IndirectOffsetOnAxis(ap=put_idx[:, t.slot, u:u + 1], axis=0),
                                          in_=put[:, t.slot, u, :], in_offset=None, compute_op=ALU.add)\
                        .then_inc(added[t.slot], 16)

            def landed(t):
                gp.wait_ge(added[t.slot], 16 * U * (t.uses + 1))
                gp.sem_inc(drained, 1)

            turns(gp, GROUPS, RING, lambda t: gather(t, x[:, :], got_x), lead=3)

            types = node_type.rearrange("(n a) -> n a", a=1)
            got_t = got_type[:, :, :].rearrange("p s (u a) -> p s u a", a=1)
            gather(Turn(B_AT, RING), types, got_t)
            for i in range(RING):
                n = (CHUNKS - i + RING - 1) // RING
                gp.wait_ge(rows_stored[i], 16 * n)
            gp.wait_ge(trash_zeroed, 16)

            def turn_b(t):
                add(t, table[:, :])
                if not (isinstance(t.number, int) and t.number == GROUPS - 1):
                    gather(t.ahead(B_AT + 1), types, got_t)
                landed(t)

            turns(gp, GROUPS, RING, turn_b, lead=2, tail=1)

            gather(Turn(C_AT, RING), table[:, :], got)
            gather(Turn(C_AT + 1, RING), table[:, :], got)
            gp.wait_ge(sums_zeroed, 16 * (FULL_CHUNKS + 2))

            def turn_c(t):
                add(t.ahead(GROUPS), sums[:, :])
                if not (isinstance(t.number, int) and t.number >= GROUPS - 2):
                    gather(t.ahead(C_AT + 2), table[:, :], got)
                landed(t.ahead(GROUPS))

            turns(gp, GROUPS, RING, turn_c, lead=2, tail=3)
            gp.sem_inc(all_added, 1)

            def agg_over_tot(t):
                n = parts(t.number)
                gp.wait_ge(t_inv_ready, t.number + 1)
                gp.tensor_tensor(t_s[0:n, t.slot, :, 0:H], t_s[0:n, t.slot, :, 0:H], wide(t_inv[0:n, t.slot], H), ALU.mult)\
                    .then_inc(t_agg, 1)

            def finish(t):
                n = parts(t.number)
                st = Steps(gp, t_pstep, 2 * t.number)
                st.add(gp.tensor_tensor(t_x[0:n, t.slot, :, 0:H], t_x[0:n, t.slot, :, 0:H], rows(beta_b[0:n], NR), ALU.add))
                gp.wait_ge(t_norm, t.number + 1)
                st.add(gp.tensor_tensor(t_y[0:n, t.slot], t_y[0:n, t.slot], rows(gamma_b[0:n], NR), ALU.mult))
                st.wait()
                gp.tensor_tensor(t_y[0:n, t.slot], t_y[0:n, t.slot], t_x[0:n, t.slot, :, 0:H], ALU.add).then_inc(t_out, 1)

            def last_turn(t):
                if not (isinstance(t.number, int) and t.number >= CHUNKS):
                    agg_over_tot(t)
                if not (isinstance(t.number, int) and t.number < 2):
                    finish(t.ahead(-2))

            turns(gp, CHUNKS + 2, TRING, last_turn, lead=3, tail=3)

        @block.vector
        def _(dve):
            v = nc.vector
            st = Steps(dve, setup_step, 0)
            st.add(v.memset(ew[:, FULL:TILES], 0.0))
            st.wait()
            dve.sem_inc(pads_set, 1)
            v.memset(half_pi[:, :], 3.141592653589793 / 2)
            v.memset(msg[:, :, :, :], 0.0)
            v.memset(attr_in[:, :, :, :], 0.0)
            v.memset(attrT[:, :], 1.0)
            st.add(v.memset(hidden[:, :], 1.0))
            dve.wait_ge(order_loaded, 16 * 6)
            v.tensor_copy(slot_idx[:, 0, :], order[:, 0:U]).then_inc(idx_ready, 1)
            v.tensor_copy(slot_idx[:, 1, :], order[:, U:2 * U]).then_inc(idx_ready, 1)
            dve.wait_ge(keys_loaded, 16 * 4)
            dve.wait_ge(const_set, 8)
            st.add(v.tensor_copy(keys[:, :, :], keys_i[:, :, :]))
            st.add(v.tensor_copy(trash[:, :], trash_i[:, :]))
            st.wait()
            for n in range(2):
                st.add(v.tensor_tensor(rel[:, n], keys[:, n, :].rearrange("p (g u) -> p g u", u=U),
                                       rows(trash[:, :], GROUPS), ALU.subtract))
            dve.wait_ge(ew_loaded, 32)
            st.add(v.tensor_scalar(cw_t[:, :], ew[:, :], 0.5 / CUTOFF, ROUND, ALU.mult, ALU.add))
            st.wait()
            st.add(v.tensor_scalar(cw_t[:, :], cw_t[:, :], -ROUND, None, ALU.add))
            st.wait()
            st.add(v.scalar_tensor_tensor(out=cw_t[:, :], in0=ew[:, :], scalar=0.5 / CUTOFF, in1=cw_t[:, :],
                                          op0=ALU.mult, op1=ALU.subtract))
            st.wait()
            st.add(v.tensor_scalar(cutoff_w[:, :], cw_t[:, :], -1.0, None, ALU.mult))
            st.wait()
            v.tensor_tensor(cw_t[:, :], cw_t[:, :], cutoff_w[:, :], ALU.max).then_inc(cw_angle, 1)
            dve.wait_ge(cw_sin, 1)
            st.add(v.tensor_scalar(cw_t[:, :], cw_t[:, :], 0.5, 0.5, ALU.mult, ALU.add))
            st.add(v.tensor_scalar(cutoff_w[:, :], ew[:, :], CUTOFF, None, ALU.is_lt))
            st.wait()
            st.add(v.tensor_tensor(cutoff_w[:, :], cutoff_w[:, :], cw_t[:, :], ALU.mult))
            dve.wait_ge(w_turned, 3)
            v.tensor_copy(w1T[0:R, :], bank[4][0:R, 0:H])
            v.tensor_copy(w2T[0:H, :], bank[4][0:H, 64:64 + H])
            v.tensor_copy(embT[:, :], bank[4][0:DIM, 128:128 + KINDS]).then_inc(w_copied, 1)
            dve.wait_ge(w_turned, 4)
            v.tensor_copy(adapted[:, :], bank[5][0:DIM, 0:KINDS]).then_inc(w_copied, 1)
            dve.wait_ge(w_turned, 5)
            v.tensor_copy(logits[:, :], bank[6][0:KINDS, 0:KINDS]).then_inc(w_copied, 1)
            st.wait()
            dve.wait_ge(w_copied, 3)

            def next_idx(t):
                if not (isinstance(t.number, int) and t.number + RING >= 3 * GROUPS):
                    v.tensor_scalar(slot_idx[:, t.slot, :], order[:, bass.ds(U * (t.number + RING), U)], 0.0, None, ALU.add)\
                        .then_inc(idx_ready, 1)

            def arrived(t):
                dve.wait_ge(gathered[t.slot], 16 * U * (t.uses + 1))

            A_STEPS = 6

            def turn_a(t):
                st = Steps(dve, a_step, A_STEPS * t.number)
                xg = got_x[:, t.slot]
                arrived(t)
                st.add(v.tensor_reduce(s4[:, :], xg, AX.X, ALU.add))
                st.wait()
                st.add(v.tensor_scalar(m4[:, :], s4[:, :], 1.0 / H, None, ALU.mult))
                st.wait()
                st.add(v.tensor_tensor(dev[:, t.slot], xg, wide(m4[:, :], H), ALU.subtract))
                st.wait()
                next_idx(t)
                v.tensor_scalar(group(dev0, t.number), dev[:, t.slot], 0.0, None, ALU.max)
                st.add(v.tensor_tensor(sq4[:, :, :], dev[:, t.slot], dev[:, t.slot], ALU.mult))
                st.wait()
                st.add(v.tensor_reduce(v4[:, :], sq4[:, :, :], AX.X, ALU.add))
                st.wait()
                st.add(v.tensor_scalar(group(var0, t.number), v4[:, :], 1.0 / H, EPS, ALU.mult, ALU.add))
                assert st.n == A_STEPS

            turns(dve, GROUPS, RING, turn_a, lead=3)
            dve.wait_ge(a_step, A_STEPS * GROUPS)
            v.sem_inc(var0_ready, 1)
            dve.wait_ge(sd0_ready, 1)
            b0 = Steps(dve, b_step, 0)
            b0.add(v.reciprocal(rw[:, :], var0[:, :]))
            b0.wait()
            b0.add(v.tensor_tensor(rw[:, :], rw[:, :], ew[:, :], ALU.mult))
            b0.wait()

            def take_keys(t, n, g):
                if not t.slot_is_new:
                    dve.wait_ge(summed, t.number - 1)
                v.tensor_scalar(key4[:, t.slot, :], group(keys[:, n, :], g), 0.0, None, ALU.add).then_inc(key4_ready, 1)

            def compare(t, g, n, st):
                dve.wait_ge(keys_turned, t.number + 1)
                for j in range(U):
                    last = v.scalar_tensor_tensor(out=same[:, t.slot, SPAN_AT[j]:SPAN_AT[j] + SPAN[j]],
                                                  in0=ps_key[t.slot][:, j * P:U * P], scalar=key4[:, t.slot, j:j + 1],
                                                  in1=upto[:, 0:SPAN[j]], op0=ALU.is_equal, op1=ALU.mult,
                                                  accum_out=count[:, t.slot, j:j + 1])
                last.then_inc(same_ready, 1)
                dve.wait_ge(same_ready, t.number + 1)
                st.add(v.tensor_scalar(last4[:, :], count[:, t.slot], 1.0, None, ALU.is_equal))
                st.wait()
                st.add(v.tensor_tensor(off4[:, :], rel[:, n, bass.ds(g, 1), :].rearrange("p a u -> p (a u)"), last4[:, :], ALU.mult))
                if not t.slot_is_new:
                    dve.wait_ge(drained, t.number - 1)
                st.wait()
                v.tensor_tensor(put_idx[:, t.slot], off4[:, :], trash[:, :], ALU.add).then_inc(put_idx_ready, 1)

            B_STEPS = 3

            def turn_b(t):
                g = t.number
                st = Steps(dve, b_step, 2 + B_STEPS * g)
                take_keys(t, 0, g)
                v.tensor_tensor(msg[:, t.slot, :, 0:H], group(dev0, g), wide(group(rw, g), H), ALU.mult)
                compare(t, g, 0, st)
                dve.wait_ge(sig_ready, g + 1)
                v.tensor_tensor(hidden[0:H, :], ps_hid[0:H, :], sig[:, :], ALU.mult).then_inc(hidden_ready, 1)
                m = t.ahead(B_AT)
                arrived(m)
                st.add(v.tensor_scalar(group(type_src, g), got_type[:, m.slot], 0.0, None, ALU.add))
                st.wait()
                next_idx(m)
                assert st.n == B_STEPS

            turns(dve, GROUPS, RING, turn_b, lead=3)
            dve.wait_ge(b_step, 2 + B_STEPS * GROUPS)
            dve.wait_ge(gate_copied, GROUPS)

            def turn_c(t):
                g = t.number
                st = Steps(dve, c_step, C_STEPS * g)
                m, n = t.ahead(C_AT), t.ahead(GROUPS)
                rowsg = got[:, m.slot]
                xg = got[:, m.slot, :, 0:H]
                v.tensor_scalar(type4[:, :], group(type_src, g), 0.0, None, ALU.add).then_inc(type4_ready, 1)
                take_keys(n, 1, g)
                arrived(m)
                st.add(v.tensor_reduce(s4[:, :], xg, AX.X, ALU.add))
                st.wait()
                st.add(v.tensor_scalar(m4[:, :], s4[:, :], 1.0 / H, None, ALU.mult))
                st.wait()
                st.add(v.tensor_tensor(dev[:, m.slot], xg, wide(m4[:, :], H), ALU.subtract))
                st.wait()
                st.add(v.tensor_tensor(sq4[:, :, :], dev[:, m.slot], dev[:, m.slot], ALU.mult))
                st.wait()
                st.add(v.tensor_reduce(v4[:, :], sq4[:, :, :], AX.X, ALU.add))
                st.wait()
                v.tensor_scalar(ve4[:, m.slot], v4[:, :], 1.0 / H, EPS, ALU.mult, ALU.add).then_inc(var_ready, 1)
                dve.wait_ge(types_turned, g + 1)
                v.tensor_scalar(onehot[:, :], ps_type[0:KINDS, :], kind_col[0:KINDS, 0:1], None, ALU.is_equal)\
                    .then_inc(onehot_ready, 1)
                compare(n, g, 1, st)
                dve.wait_ge(logit_done, g + 1)
                for u in range(U):
                    last = v.scalar_tensor_tensor(out=hit[:, u, :], in0=kind_row[:, :], scalar=rowsg[:, u, H + 1:H + 2],
                                                  in1=ps_logit[:, u * KINDS:(u + 1) * KINDS], op0=ALU.is_equal, op1=ALU.mult,
                                                  accum_out=lg4[:, u:u + 1])
                st.add(last)
                dve.wait_ge(sd_ready, g + 1)
                st.add(v.reciprocal(cf4[:, :], sd4[:, m.slot]))
                st.wait()
                st.add(v.tensor_tensor(cf4[:, :], cf4[:, :], group(cutoff_w, g), ALU.mult))
                st.wait()
                st.add(v.tensor_tensor(cf4[:, :], cf4[:, :], rowsg[:, :, H], ALU.mult))
                st.add(v.tensor_tensor(gl4[:, :, :], group(gate, g), wide(lg4[:, :], H), ALU.add))
                v.tensor_scalar(msg[:, n.slot, :, H], rowsg[:, :, H], 0.0, None, ALU.add)
                st.wait()
                st.add(v.scalar_tensor_tensor(out=dev[:, m.slot], in0=dev[:, m.slot], scalar=0.0, in1=wide(cf4[:, :], H),
                                              op0=ALU.max, op1=ALU.mult))
                st.wait()
                st.add(v.tensor_tensor(msg[:, n.slot, :, 0:H], gl4[:, :, :], dev[:, m.slot], ALU.mult))
                st.wait()
                next_idx(m)
                assert st.n == C_STEPS

            turns(dve, GROUPS, RING, turn_c, lead=3, tail=2)
            dve.wait_ge(c_step, C_STEPS * GROUPS)

            T_STEPS = 12

            def first_part(t, st):
                n = parts(t.number)
                dve.wait_ge(t_loaded[t.slot], 32 * (t.uses + 1))
                xt = t_x[0:n, t.slot, :, 0:H]
                st.add(v.tensor_scalar(t_inv[0:n, t.slot], t_s[0:n, t.slot, :, H], 1e-8, None, ALU.max))
                st.add(v.tensor_reduce(t_m[0:n, :], xt, AX.X, ALU.add))
                st.wait()
                v.reciprocal(t_inv[0:n, t.slot], t_inv[0:n, t.slot]).then_inc(t_inv_ready, 1)
                st.add(v.tensor_scalar(t_m[0:n, :], t_m[0:n, :], 1.0 / H, None, ALU.mult))
                st.wait()
                v.tensor_tensor(t_d[0:n, t.slot], xt, wide(t_m[0:n, :], H), ALU.subtract).then_inc(t_dev, 1)

            def var_of(t, st, square_sem, square, var, var_sem):
                n = parts(t.number)
                dve.wait_ge(square_sem, t.number + 1)
                st.add(v.tensor_reduce(var[0:n, t.slot], square[0:n, t.slot], AX.X, ALU.add))
                st.wait()
                v.tensor_scalar(var[0:n, t.slot], var[0:n, t.slot], 1.0 / H, EPS, ALU.mult, ALU.add).then_inc(var_sem, 1)

            def middle_part(t, st):
                n = parts(t.number)
                y = t_y[0:n, t.slot]
                dve.wait_ge(t_std1, t.number + 1)
                st.add(v.reciprocal(t_sd1[0:n, t.slot], t_sd1[0:n, t.slot]))
                if not t.slot_is_new:
                    dve.wait_ge(t_stored[t.slot], 16 * t.uses)
                st.wait()
                st.add(v.scalar_tensor_tensor(out=y, in0=t_d[0:n, t.slot], scalar=0.0, in1=wide(t_sd1[0:n, t.slot], H),
                                              op0=ALU.max, op1=ALU.mult))
                dve.wait_ge(t_agg, t.number + 1)
                st.wait()
                st.add(v.tensor_tensor(y, y, t_s[0:n, t.slot, :, 0:H], ALU.add))
                st.wait()
                st.add(v.tensor_reduce(t_m[0:n, :], y, AX.X, ALU.add))
                st.wait()
                st.add(v.tensor_scalar(t_m[0:n, :], t_m[0:n, :], 1.0 / H, None, ALU.mult))
                st.wait()
                v.tensor_tensor(y, y, wide(t_m[0:n, :], H), ALU.subtract).then_inc(t_dev2, 1)

            def end_part(t, st):
                n = parts(t.number)
                dve.wait_ge(t_std2, t.number + 1)
                st.add(v.reciprocal(t_sd2[0:n, t.slot], t_sd2[0:n, t.slot]))
                st.wait()
                v.tensor_tensor(t_y[0:n, t.slot], t_y[0:n, t.slot], wide(t_sd2[0:n, t.slot], H), ALU.mult).then_inc(t_norm, 1)

            def last_turn(t):
                known = isinstance(t.number, int)
                c = t.number if known else None
                done = {0: 0, 1: 3, 2: 10}
                if known:
                    first = 3 * min(c, CHUNKS) + 6 * min(max(c - 1, 0), CHUNKS) + 2 * min(max(c - 2, 0), CHUNKS)
                else:
                    first = 11 * t.number - 10
                st = Steps(dve, t_step, first)
                has = lambda back: not known or 0 <= c - back < CHUNKS
                if has(1):
                    var_of(t.ahead(-1), st, t_sq1, t_q1, t_v1, t_var1)
                if has(2):
                    var_of(t.ahead(-2), st, t_sq2, t_q2, t_v2, t_var2)
                if has(0):
                    first_part(t, st)
                if has(1):
                    middle_part(t.ahead(-1), st)
                if has(2):
                    end_part(t.ahead(-2), st)

            turns(dve, CHUNKS + 2, TRING, last_turn, lead=3, tail=3)

        @block.scalar
        def _(act):
            s = nc.scalar
            act.wait_ge(cw_angle, 1)
            s.activation(cw_t[:, :], cw_t[:, :], ACT.Sin, bias=half_pi[:, 0:1], scale=-2 * 3.141592653589793)\
                .then_inc(cw_sin, 1)
            act.wait_ge(nodes_loaded, 64)

            def table_turn(t):
                n = parts(t.number)
                act.wait_ge(x_loaded[t.slot], 16 * (t.uses + 1))
                if not t.slot_is_new:
                    act.wait_ge(rows_stored[t.slot], 16 * t.uses)
                hold(act)
                at = bass.ds(t.number, 1)
                s.copy(rows_out[0:n, t.slot, :, 0:H], x_in[0:n, t.slot])
                s.copy(rows_out[0:n, t.slot, :, H], vec_in[0:n, at, :].rearrange("p a r -> p (a r)"))
                s.copy(rows_out[0:n, t.slot, :, H + 1], type_in[0:n, at, :].rearrange("p a r -> p (a r)")).then_inc(rows_built, 1)

            turns(act, CHUNKS, RING, table_turn, lead=2, tail=1)
            act.wait_ge(var0_ready, 1)
            s.activation(var0[:, :], var0[:, :], ACT.Sqrt).then_inc(sd0_ready, 1)

            def copy_sums(t):
                act.wait_ge(summed, t.number + 1)
                if not t.slot_is_new:
                    act.wait_ge(drained, t.number - 1)
                s.copy(put[:, t.slot].rearrange("p u w -> p (u w)"), ps_sum[t.slot][:, 0:U * W]).then_inc(put_ready, 1)

            def turn_b(t):
                g = t.number
                act.wait_ge(attr_turned, g + 1)
                s.copy(attrT[0:R, :], ps_attr[0:R, :]).then_inc(attrT_ready, 1)
                act.wait_ge(hid_done, g + 1)
                s.activation(sig[:, :], ps_hid[0:H, :], ACT.Sigmoid).then_inc(sig_ready, 1)
                copy_sums(t)
                act.wait_ge(gate_done, g + 1)
                hold(act)
                s.copy(group(gate, g), ps_gate[:, 0:U * H].rearrange("p (u h) -> p u h", u=U)).then_inc(gate_copied, 1)

            act.wait_ge(setup_step, 2)
            turns(act, GROUPS, RING, turn_b, lead=3)

            def turn_c(t):
                g = t.number
                m = t.ahead(C_AT)
                act.wait_ge(var_ready, g + 1)
                s.activation(sd4[:, m.slot], ve4[:, m.slot], ACT.Sqrt).then_inc(sd_ready, 1)
                copy_sums(t.ahead(GROUPS))

            turns(act, GROUPS, RING, turn_c, lead=3)

            def square(t, dev_sem, dev_of, square_of, done):
                n = parts(t.number)
                act.wait_ge(dev_sem, t.number + 1)
                s.activation(square_of[0:n, t.slot], dev_of[0:n, t.slot], ACT.Square).then_inc(done, 1)

            def root(t, var_sem, var, std, done):
                n = parts(t.number)
                act.wait_ge(var_sem, t.number + 1)
                s.activation(std[0:n, t.slot], var[0:n, t.slot], ACT.Sqrt).then_inc(done, 1)

            def last_turn(t):
                known = isinstance(t.number, int)
                has = lambda back: not known or 0 <= t.number - back < CHUNKS
                if has(1):
                    root(t.ahead(-1), t_var1, t_v1, t_sd1, t_std1)
                if has(2):
                    root(t.ahead(-2), t_var2, t_v2, t_sd2, t_std2)
                if has(0):
                    square(t, t_dev, t_d, t_q1, t_sq1)
                if has(1):
                    square(t.ahead(-1), t_dev2, t_y, t_q2, t_sq2)

            turns(act, CHUNKS + 2, TRING, last_turn, lead=3, tail=3)

        @block.tensor
        def _(pe):
            te = nc.tensor
            pe.wait_ge(const_set, 8)
            pe.wait_ge(weights_loaded, 16 * 8)
            te.transpose(bank[4][0:R, 0:H], w1_in[:, :], ident[0:H, 0:H]).then_inc(w_turned, 1)
            te.transpose(bank[4][0:H, 64:64 + H], w2_in[:, :], ident[0:H, 0:H]).then_inc(w_turned, 1)
            te.transpose(bank[4][0:DIM, 128:128 + KINDS], emb_in[:, :], ident[0:KINDS, 0:KINDS]).then_inc(w_turned, 1)
            pe.wait_ge(w_copied, 1)
            te.matmul(bank[5][0:DIM, 0:KINDS], adapt_in[:, :], embT[:, :], start=True, stop=True).then_inc(w_turned, 1)
            pe.wait_ge(w_copied, 2)
            te.matmul(bank[6][0:KINDS, 0:KINDS], adapted[:, :], embT[:, :], start=True, stop=True).then_inc(w_turned, 1)
            pe.wait_ge(w_copied, 3)

            def turn_keys(t):
                pe.wait_ge(key4_ready, t.number + 1)
                if not t.slot_is_new:
                    pe.wait_ge(same_ready, t.number - 1)
                hold(pe)
                for u in range(U):
                    last = te.transpose(ps_key[t.slot][:, u * P:(u + 1) * P], key4[:, t.slot, u:u + 1].broadcast_to([P, P]), ident[:, :])
                last.then_inc(keys_turned, 1)

            def sum_equal(t):
                pe.wait_ge(same_ready, t.number + 1)
                if not t.slot_is_new:
                    pe.wait_ge(put_ready, t.number - 1)
                hold(pe)
                for i in range(U):
                    for j in range(i + 1):
                        at = SPAN_AT[j] + (i - j) * P
                        last = te.matmul(ps_sum[t.slot][:, i * W:(i + 1) * W], same[:, t.slot, at:at + P], msg[:, t.slot, j],
                                         start=(j == 0), stop=(j == i))
                last.then_inc(summed, 1)

            def turn_b(t):
                g = t.number
                turn_keys(t)
                first = isinstance(g, int) and g == 0
                if isinstance(g, int) and g == GROUPS - 1:
                    pe.wait_ge(attr_loaded[t.slot], 16 * (t.uses + 2))
                else:
                    pe.wait_ge(attr_loaded[t.slot], 16 * (t.uses + 1))
                if not first:
                    pe.wait_ge(attrT_ready, g)
                hold(pe)
                for u in range(U):
                    last = te.transpose(ps_attr[0:R, u * P:(u + 1) * P], attr_in[:, t.slot, u, :], ident[:, :])
                last.then_inc(attr_turned, 1)
                pe.wait_ge(attrT_ready, g + 1)
                if not first:
                    pe.wait_ge(hidden_ready, g)
                hold(pe)
                te.matmul(ps_hid[0:H, :], w1T[:, :], attrT[0:R + 1, :], start=True, stop=True).then_inc(hid_done, 1)
                sum_equal(t)
                pe.wait_ge(hidden_ready, g + 1)
                if not first:
                    pe.wait_ge(gate_copied, g)
                hold(pe)
                for u in range(U):
                    last = te.matmul(ps_gate[:, u * H:(u + 1) * H], hidden[0:H + 1, u * P:(u + 1) * P], w2T[:, :],
                                     start=True, stop=True)
                last.then_inc(gate_done, 1)

            turns(pe, GROUPS, RING, turn_b, lead=2, tail=1)

            pe.wait_ge(gate_copied, GROUPS)

            def turn_c(t):
                g = t.number
                first = isinstance(g, int) and g == 0
                pe.wait_ge(type4_ready, g + 1)
                if not first:
                    pe.wait_ge(onehot_ready, g)
                hold(pe)
                for u in range(U):
                    last = te.transpose(ps_type[:, u * P:(u + 1) * P], type4[:, u:u + 1].broadcast_to([P, P]), ident[:, :])
                last.then_inc(types_turned, 1)
                turn_keys(t.ahead(GROUPS))
                pe.wait_ge(onehot_ready, g + 1)
                if not first:
                    pe.wait_ge(c_step, C_STEPS * g)
                hold(pe)
                for u in range(U):
                    last = te.matmul(ps_logit[:, u * KINDS:(u + 1) * KINDS], onehot[:, u * P:(u + 1) * P], logits[:, :],
                                     start=True, stop=True)
                last.then_inc(logit_done, 1)
                pe.wait_ge(c_step, C_STEPS * (g + 1))
                sum_equal(t.ahead(GROUPS))

            turns(pe, GROUPS, RING, turn_c, lead=3)


_INS = ['x', 'src', 'dst', 'edge_attr_40', 'edge_weight', 'node_type_119', 'node_vec', 'L1_gnn_W1', 'L1_gnn_b1',
        'L1_gnn_W2', 'L1_gnn_b2', 'L1_gnn_emb', 'L1_gnn_adaptW', 'L1_gnn_gamma', 'L1_gnn_beta']


def kernel(**inputs):
    import numpy as _np
    import concourse.bacc as _bacc
    from concourse import mybir as _mybir
    from concourse.bass_utils import run_bass_kernel_spmd as _run

    nc = _bacc.Bacc("TRN2", target_bir_lowering=False, num_devices=1)
    arrays, args = {}, []
    for name in _INS:
        a = _np.ascontiguousarray(inputs[name])
        arrays[f"in_{name}_dram"] = a
        args.append(nc.dram_tensor(f"in_{name}_dram", a.shape, _mybir.dt.from_np(a.dtype), kind="ExternalInput").ap())
    shape = inputs['x'].shape
    args.append(nc.dram_tensor("out_0_dram", shape, _mybir.dt.from_np(_np.dtype('float32')), kind="ExternalOutput").ap())
    gnn_kernel(nc, *args)
    r = _run(nc, [arrays], core_ids=[0])
    return r.results[0]["out_0_dram"]
```

```python
import concourse.bass as bass
from concourse import mybir
from contextlib import ExitStack


class Turn:

    def __init__(self, base, ring, k=None):
        self.base, self.ring, self.k = base, ring, k

    @property
    def number(self):
        return self.base if self.k is None else self.base + self.ring * self.k

    @property
    def slot(self):
        return self.base % self.ring

    @property
    def uses(self):
        return self.base // self.ring if self.k is None else self.base // self.ring + self.k

    @property
    def half(self):
        return self.base % 2

    @property
    def half_is_new(self):
        return self.k is None and self.base < 2

    def ahead(self, turns):
        return Turn(self.base + turns, self.ring, self.k)

    @property
    def slot_is_new(self):
        return self.k is None and self.base < self.ring


def turns(eng, count, ring, body, lead, tail=0):
    rounds, rest = divmod(count - lead - tail, ring)
    assert rest == 0 and lead >= ring
    for n in range(lead):
        body(Turn(n, ring))
    with eng.Fori(0, rounds) as k:
        for r in range(ring):
            body(Turn(lead + r, ring, k))
    for n in range(count - tail, count):
        body(Turn(n, ring))


def known(t, least, most):
    return t.k is not None or least <= t.base < most


class Steps:

    def __init__(self, eng, sem, first):
        self.eng, self.sem, self.first, self.n = eng, sem, first, 0

    def add(self, instruction):
        instruction.then_inc(self.sem, 1)
        self.n += 1

    def wait(self):
        self.eng.wait_ge(self.sem, self.first + self.n)


def gnn_kernel(nc, x, src, dst, edge_attr, edge_weight, node_type, node_vec, W1, b1, W2, b2, emb, adaptW, gamma,
               beta, out):
    fp32 = mybir.dt.float32
    i32 = mybir.dt.int32
    ALU = mybir.AluOpType
    ACT = mybir.ActivationFunctionType
    AX = mybir.AxisListType

    P = 128
    N, H = x.shape
    E, R = edge_attr.shape
    KINDS, DIM = emb.shape
    EPS = 1e-5
    CUTOFF = 6.0
    ROUND = 1.5 * 2.0 ** 23

    FULL = E // P
    REM = E - P * FULL
    TILES = FULL + 1
    U = 4
    GROUPS = TILES // U
    assert GROUPS * U == TILES
    RING = 4
    W = H + 2
    TRASH = N
    ROWS = N + U * P
    SPAN = [(U - j) * P for j in range(U)]
    SPAN_AT = [sum(SPAN[:j]) for j in range(U)]

    NR = 16
    CHUNK = P * NR
    FULL_CHUNKS = N // CHUNK
    LAST_P = (N - FULL_CHUNKS * CHUNK) // NR
    CHUNKS = FULL_CHUNKS + 1
    assert FULL_CHUNKS * CHUNK + LAST_P * NR == N
    TRING = 6
    HALF = NR // 2
    PAIR = 2 * H
    BLOCKS = HALF // 2

    table = nc.dram_tensor("node_table", (ROWS, W), fp32, kind="Internal").ap()
    sums = nc.dram_tensor("edge_sums", (ROWS, W), fp32, kind="Internal").ap()
    hs = nc.dram_tensor("hidden_nodes", (N, H), fp32, kind="Internal").ap()

    def chunk(t, c):
        if isinstance(c, int) and c == FULL_CHUNKS:
            return t[FULL_CHUNKS * CHUNK:N].rearrange("(p r) f -> p (r f)", r=NR)
        v = t[0:FULL_CHUNKS * CHUNK].rearrange("(c p r) f -> c p (r f)", p=P, r=NR)
        return v[bass.ds(c, 1)].rearrange("a p f -> (a p) f")

    def parts(c):
        return LAST_P if isinstance(c, int) and c == FULL_CHUNKS else P

    ctx = ExitStack()
    with ctx:
        def sb(name, shape, dt=fp32):
            return ctx.enter_context(nc.sbuf_tensor(name, shape, dt))

        def sem(name):
            return ctx.enter_context(nc.semaphore(name))

        order = sb("order", [P, 3 * TILES], i32)
        keys_i = sb("keys_i", [P, 2, TILES], i32)
        keys = sb("keys", [P, 2 * TILES])
        rel = sb("rel", [P, 2 * TILES])
        trash_i = sb("trash_i", [P, U], i32)
        trash = sb("trash", [P, U])
        ew = sb("ew", [P, TILES])
        cutoff_w = sb("cutoff_w", [P, TILES])
        cw_t = sb("cw_t", [P, TILES])
        half_pi = sb("half_pi", [P, 1])
        early = sb("early", [P, TILES * H + RING * NR * (H + W)])
        dev0 = early[:, 0:TILES * H].rearrange("p (t h) -> p t h", h=H)
        gate = sb("gate", [P, TILES, H])
        var0 = sb("var0", [P, TILES])
        rw = sb("rw", [P, TILES])
        type_src = sb("type_src", [P, TILES])
        ident = sb("ident", [P, P])
        upto = sb("upto", [P, U * P])
        kind_row = sb("kind_row", [P, KINDS])
        kind_col = sb("kind_col", [P, 1])
        zeros = sb("zeros", [P, NR * W])
        gamma_b = sb("gamma_b", [P, H])
        beta_b = sb("beta_b", [P, H])
        w1_in = sb("w1_in", [H, R])
        w2_in = sb("w2_in", [H, H])
        emb_in = sb("emb_in", [KINDS, DIM])
        adapt_in = sb("adapt_in", [DIM, DIM])
        w1T = sb("w1T", [R + 1, H])
        w2T = sb("w2T", [H + 1, H])
        embT = sb("embT", [DIM, KINDS])
        adapted = sb("adapted", [DIM, KINDS])
        logits = sb("logits", [KINDS, KINDS])
        vec_in = sb("vec_in", [P, CHUNKS, NR])
        type_in = sb("type_in", [P, CHUNKS, NR], i32)
        at = TILES * H
        x_in = early[:, at:at + RING * NR * H].rearrange("p (s r h) -> p s r h", s=RING, h=H)
        at += RING * NR * H
        rows_out = early[:, at:at + RING * NR * W].rearrange("p (s r w) -> p s r w", s=RING, w=W)
        slot_idx = sb("slot_idx", [P, RING, U], i32)
        got = sb("got", [P, RING, U, W])
        got_x = sb("got_x", [P, RING, U, H])
        got_type = sb("got_type", [P, RING, U], i32)
        s4 = sb("s4", [P, U])
        m4 = sb("m4", [P, U])
        v4 = sb("v4", [P, U])
        sq4 = sb("sq4", [P, U, H])
        dev = sb("dev", [P, RING, U, H])
        sd4 = sb("sd4", [P, RING, U])
        ve4 = sb("ve4", [P, RING, U])
        lg4 = sb("lg4", [P, U])
        cf4 = sb("cf4", [P, U])
        gl4 = sb("gl4", [P, U, H])
        hit = sb("hit", [P, U, KINDS])
        key4 = sb("key4", [P, 2, U])
        type4 = sb("type4", [P, U])
        onehot = sb("onehot", [KINDS, U * P])
        msg = sb("msg", [P, 2, U, W])
        same = sb("same", [P, 2, sum(SPAN)])
        count = sb("count", [P, 2, U])
        last4 = sb("last4", [P, U])
        off4 = sb("off4", [P, U])
        put_idx = sb("put_idx", [P, 2, U], i32)
        put = sb("put", [P, 2, U, W])
        attr_in = sb("attr_in", [P, RING, U, R])
        attrT = sb("attrT", [64, U * P])
        sig = sb("sig", [H, U * P])
        hidden = sb("hidden", [64, U * P])
        center = sb("center", [PAIR, 2, PAIR])
        center_w = sb("center_w", [W + H, PAIR])
        c_x = sb("c_x", [P, 2, NR, W])
        c_q = sb("c_q", [P, NR, H])
        c_h = sb("c_h", [P, 2, NR, H])
        c_v = sb("c_v", [P, NR])
        c_sd = sb("c_sd", [P, NR])
        c_r = sb("c_r", [P, NR])
        xT = sb("xT", [W + H, 2, BLOCKS * P])
        assert TRING * NR * (2 * W) <= TILES * H + RING * NR * (H + W) and TRING * NR * H <= TILES * H
        at = TRING * NR * W
        t_x = early[:, 0:at].rearrange("p (s r w) -> p s r w", s=TRING, w=W)
        t_s = early[:, at:2 * at].rearrange("p (s r w) -> p s r w", s=TRING, w=W)
        t_h = gate[:, 0:TRING * NR, :].rearrange("p (s r) h -> p s r h", s=TRING)
        t_inv = sb("t_inv", [P, TRING, NR])
        t_v = sb("t_v", [P, TRING, NR])
        t_sd = sb("t_sd", [P, TRING, NR])

        ps = ctx.enter_context(nc.psum_tensor("ps", [P, 8, 512], fp32))
        bank = [ps[:, i, :] for i in range(8)]
        ps_attr, ps_hid, ps_gate, ps_key, ps_sum, ps_type = bank[0:6]
        ps_logit = bank[0]
        ps_turn = [bank[1], bank[2]]
        ps_dev = [bank[6], bank[7]]
        t_turn = [bank[0], bank[1]]
        t_dev = [ps[:, 2 * i + 2:2 * i + 4, 0:2 * 2 * PAIR].rearrange("p b (i k f) -> p b i k f", i=2, k=2) for i in range(3)]

        keys_loaded = sem("keys_loaded")
        order_loaded = sem("order_loaded")
        ew_loaded = sem("ew_loaded")
        nodes_loaded = sem("nodes_loaded")
        weights_loaded = sem("weights_loaded")
        pads_set = sem("pads_set")
        const_set = sem("const_set")
        w_turned = sem("w_turned")
        w_copied = sem("w_copied")
        cw_angle = sem("cw_angle")
        cw_sin = sem("cw_sin")
        setup_step = sem("setup_step")
        setup_done = sem("setup_done")
        x_loaded = [sem(f"x_loaded{i}") for i in range(RING)]
        rows_built = sem("rows_built")
        rows_stored = [sem(f"rows_stored{i}") for i in range(RING)]
        act_step = sem("act_step")
        trash_zeroed = sem("trash_zeroed")
        sums_zeroed = sem("sums_zeroed")
        idx_ready = sem("idx_ready")
        gathered = [sem(f"gathered{i}") for i in range(RING)]
        a_step = sem("a_step")
        var0_ready = sem("var0_ready")
        sd0_ready = sem("sd0_ready")
        b_step = sem("b_step")
        c_step = sem("c_step")
        key4_ready = sem("key4_ready")
        keys_turned = sem("keys_turned")
        same_ready = sem("same_ready")
        put_idx_ready = sem("put_idx_ready")
        summed = sem("summed")
        put_ready = sem("put_ready")
        added = [sem(f"added{i}") for i in range(RING)]
        drained = sem("drained")
        attr_loaded = [sem(f"attr_loaded{i}") for i in range(RING)]
        attr_turned = sem("attr_turned")
        attrT_ready = sem("attrT_ready")
        hid_done = sem("hid_done")
        sig_ready = sem("sig_ready")
        hidden_ready = sem("hidden_ready")
        gate_done = sem("gate_done")
        gate_copied = sem("gate_copied")
        var_ready = sem("var_ready")
        sd_ready = sem("sd_ready")
        type4_ready = sem("type4_ready")
        types_turned = sem("types_turned")
        onehot_ready = sem("onehot_ready")
        logit_done = sem("logit_done")
        logit_read = sem("logit_read")
        msg_ready = sem("msg_ready")
        center_set = sem("center_set")
        c_loaded = [sem(f"c_loaded{i}") for i in range(2)]
        c_turned = sem("c_turned")
        c_copied = sem("c_copied")
        c_centered = sem("c_centered")
        c_squared = sem("c_squared")
        c_var = sem("c_var")
        c_std = sem("c_std")
        c_h_ready = sem("c_h_ready")
        c_stored = [sem(f"c_stored{i}") for i in range(2)]
        all_added = sem("all_added")
        passed = sem("passed")
        t_loaded = [sem(f"t_loaded{i}") for i in range(TRING)]
        t_step = sem("t_step")
        t_inv_ready = sem("t_inv_ready")
        t_agg = sem("t_agg")
        t_xb = sem("t_xb")
        t_x2 = sem("t_x2")
        t_turned = sem("t_turned")
        t_copied = sem("t_copied")
        t_centered = sem("t_centered")
        t_split = sem("t_split")
        t_var = sem("t_var")
        t_std = sem("t_std")
        t_out = sem("t_out")
        t_stored = [sem(f"t_stored{i}") for i in range(TRING)]

        block = ctx.enter_context(nc.Block())

        def hold(eng):
            eng.sem_inc(passed, 1)

        def wide(ap, n):
            return ap.unsqueeze(2).broadcast_to([ap.shape[0], ap.shape[1], n])

        def rows(ap, k):
            return ap.unsqueeze(1).broadcast_to([ap.shape[0], k, ap.shape[1]])

        def group(ap, g):
            return ap[:, bass.ds(U * g, U)]

        B_AT = GROUPS
        C_AT = 2 * GROUPS
        assert CHUNKS == GROUPS

        @block.sync
        def _(sp):
            def by_edge(a):
                return a[0:P * FULL].rearrange("(p t) -> p t", p=P)

            def rest(a):
                return a[P * FULL:E].rearrange("(p t) -> p t", t=1)

            sp.wait_ge(pads_set, 3)
            for n, a in enumerate((src, src, dst)):
                sp.dma_start(order[:, n * TILES:n * TILES + FULL], by_edge(a)).then_inc(order_loaded, 16)
                sp.dma_start(order[0:REM, n * TILES + FULL:(n + 1) * TILES], rest(a)).then_inc(order_loaded, 16)
            for n, a in enumerate((dst, src)):
                sp.dma_start(keys_i[:, n, 0:FULL], by_edge(a)).then_inc(keys_loaded, 16)
                sp.dma_start(keys_i[0:REM, n, FULL:TILES], rest(a)).then_inc(keys_loaded, 16)
            sp.dma_start(ew[:, 0:FULL], by_edge(edge_weight)).then_inc(ew_loaded, 16)
            sp.dma_start(ew[0:REM, FULL:TILES], rest(edge_weight)).then_inc(ew_loaded, 16)
            for t, a in ((vec_in, node_vec), (type_in, node_type)):
                sp.dma_start(t[:, 0:FULL_CHUNKS, :], a[0:FULL_CHUNKS * CHUNK].rearrange("(c p r) -> p c r", p=P, r=NR))\
                    .then_inc(nodes_loaded, 16)
                sp.dma_start(t[0:LAST_P, FULL_CHUNKS, :], a[FULL_CHUNKS * CHUNK:N].rearrange("(p r) -> p r", r=NR))\
                    .then_inc(nodes_loaded, 16)

            def load_x(t):
                sp.dma_start(x_in[0:parts(t.number), t.slot].rearrange("p r f -> p (r f)"), chunk(x, t.number))\
                    .then_inc(x_loaded[t.slot], 16)

            def store_rows(t):
                sp.wait_ge(rows_built, t.number + 1)
                sp.dma_start(chunk(table, t.number), rows_out[0:parts(t.number), t.slot].rearrange("p r f -> p (r f)"))\
                    .then_inc(rows_stored[t.slot], 16)

            def load_attr(t):
                g = t.number
                if isinstance(g, int) and g == GROUPS - 1:
                    sp.dma_start(attr_in[:, t.slot, 0:U - 1, :],
                                 edge_attr[0:P * FULL].rearrange("(p t) r -> p t r", p=P)[:, U * g:U * g + U - 1, :])\
                        .then_inc(attr_loaded[t.slot], 16)
                    sp.dma_start(attr_in[0:REM, t.slot, U - 1, :], edge_attr[P * FULL:E]).then_inc(attr_loaded[t.slot], 16)
                else:
                    sp.dma_start(attr_in[:, t.slot, :, :],
                                 edge_attr[0:P * FULL].rearrange("(p t) r -> p t r", p=P)[:, bass.ds(U * g, U), :])\
                        .then_inc(attr_loaded[t.slot], 16)

            for n in range(RING - 1):
                load_x(Turn(n, RING))
                load_attr(Turn(n, RING))
            for a, w in ((w1_in, W1), (w2_in, W2), (emb_in, emb), (adapt_in, adaptW)):
                sp.dma_start(a[:, :], w[:, :]).then_inc(weights_loaded, 16)
            sp.dma_start(w1T[R:R + 1, :], b1.rearrange("(a h) -> a h", a=1)).then_inc(weights_loaded, 16)
            sp.dma_start(w2T[H:H + 1, :], b2.rearrange("(a h) -> a h", a=1)).then_inc(weights_loaded, 16)
            sp.dma_start(gamma_b[:, :], gamma.rearrange("(a h) -> a h", a=1).broadcast_to([P, H])).then_inc(weights_loaded, 16)
            sp.dma_start(beta_b[:, :], beta.rearrange("(a h) -> a h", a=1).broadcast_to([P, H])).then_inc(weights_loaded, 16)

            def table_turn(t):
                a = t.ahead(RING - 1)
                if known(a, 0, CHUNKS):
                    if not a.slot_is_new:
                        sp.wait_ge(rows_built, t.number)
                        sp.wait_ge(attr_turned, t.number)
                    load_x(a)
                    load_attr(a)
                store_rows(t)

            turns(sp, CHUNKS, RING, table_turn, lead=5, tail=4)

            sp.wait_ge(const_set, 4)
            sp.dma_start(table[N:ROWS].rearrange("(p r) f -> p (r f)", p=P), zeros[:, 0:U * W]).then_inc(trash_zeroed, 16)
            sp.dma_start(sums[N:ROWS].rearrange("(p r) f -> p (r f)", p=P), zeros[:, 0:U * W]).then_inc(sums_zeroed, 16)
            sp.dma_start(chunk(sums, FULL_CHUNKS), zeros[0:LAST_P, :]).then_inc(sums_zeroed, 16)
            with sp.Fori(0, FULL_CHUNKS) as c:
                sp.dma_start(chunk(sums, c), zeros[:, :]).then_inc(sums_zeroed, 16)

            for i in range(RING):
                n = (CHUNKS - i + RING - 1) // RING
                sp.wait_ge(rows_stored[i], 16 * n)
            sp.wait_ge(drained, GROUPS)

            def load_c(t):
                n = parts(t.number)
                if not t.half_is_new:
                    sp.wait_ge(c_turned, 2 * (t.number - 1))
                sp.dma_start(c_x[0:n, t.half].rearrange("p r f -> p (r f)"), chunk(table, t.number))\
                    .then_inc(c_loaded[t.half], 16)

            def store_c(t):
                n = parts(t.number)
                sp.wait_ge(c_h_ready, t.number + 1)
                sp.dma_start(chunk(hs, t.number), c_h[0:n, t.half].rearrange("p r f -> p (r f)"))\
                    .then_inc(c_stored[t.half], 16)

            load_c(Turn(0, RING))

            def turn_c(t):
                if known(t, 0, CHUNKS - 1):
                    load_c(t.ahead(1))
                if known(t, 1, CHUNKS + 1):
                    store_c(t.ahead(-1))

            turns(sp, CHUNKS + 1, RING, turn_c, lead=7, tail=3)
            for i in range(2):
                sp.wait_ge(c_stored[i], 16 * ((CHUNKS - i + 1) // 2))

            sp.wait_ge(all_added, 1)

            def load_chunk(t):
                n = parts(t.number)
                for tile, a in ((t_s, sums), (t_x, table), (t_h, hs)):
                    sp.dma_start(tile[0:n, t.slot].rearrange("p r f -> p (r f)"), chunk(a, t.number))\
                        .then_inc(t_loaded[t.slot], 16)

            def store_chunk(t):
                n = parts(t.number)
                sp.wait_ge(t_out, t.number + 1)
                sp.dma_start(chunk(out, t.number), t_h[0:n, t.slot].rearrange("p r f -> p (r f)"))\
                    .then_inc(t_stored[t.slot], 16)

            def last_turn(t):
                if known(t, TRING, CHUNKS):
                    sp.wait_ge(t_stored[t.slot], 16 * t.uses)
                if known(t, 0, CHUNKS):
                    load_chunk(t)
                if known(t, TRING - 1, CHUNKS + TRING - 1):
                    store_chunk(t.ahead(1 - TRING))

            turns(sp, CHUNKS + TRING - 1, TRING, last_turn, lead=6, tail=6)
            for n in range(CHUNKS - TRING, CHUNKS):
                t = Turn(n, TRING)
                sp.wait_ge(t_stored[t.slot], 16 * (t.uses + 1))

        @block.gpsimd
        def _(gp):
            for n in range(2):
                last = gp.memset(order[:, (n + 1) * TILES - 1:(n + 1) * TILES], 0)
            last.then_inc(pads_set, 1)
            for n in range(2):
                last = gp.iota(keys_i[:, n, FULL:TILES], pattern=[[0, 1]], base=TRASH + (U - 1) * P, channel_multiplier=1)
            gp.iota(order[:, 3 * TILES - 1:3 * TILES], pattern=[[0, 1]], base=TRASH + (U - 1) * P,
                    channel_multiplier=1).then_inc(pads_set, 1)
            gp.iota(trash_i[:, :], pattern=[[P, U]], base=TRASH, channel_multiplier=1).then_inc(const_set, 1)
            gp.iota(kind_row[:, :], pattern=[[1, KINDS]], base=0, channel_multiplier=0,
                    allow_small_or_imprecise_dtypes=True).then_inc(const_set, 1)
            gp.iota(kind_col[:, :], pattern=[[0, 1]], base=0, channel_multiplier=1,
                    allow_small_or_imprecise_dtypes=True).then_inc(const_set, 1)
            gp.memset(zeros[:, :], 0.0).then_inc(const_set, 1)
            gp.memset(ident[:, :], 0.0).then_inc(const_set, 1)
            gp.memset(upto[:, :], 1.0).then_inc(const_set, 1)
            gp.wait_ge(const_set, 6)
            gp.affine_select(out=ident[:, :], in_=ident[:, :], compare_op=ALU.not_equal, fill=1.0, base=0,
                             pattern=[[-1, P]], channel_multiplier=1).then_inc(const_set, 1)
            for n, (m, step) in enumerate(((center[:, 0], H), (center_w[:, :], W))):
                same_row = m.rearrange("q (b h) -> q b h", b=2)
                gp.memset(m, -1.0 / H).then_inc(center_set, 1)
                gp.wait_ge(center_set, 4 * n + 1)
                gp.affine_select(out=same_row, in_=same_row, compare_op=ALU.is_ge, fill=0.0, base=0,
                                 pattern=[[-step, 2], [0, H]], channel_multiplier=1).then_inc(center_set, 1)
                gp.wait_ge(center_set, 4 * n + 2)
                gp.affine_select(out=same_row, in_=same_row, compare_op=ALU.is_ge, fill=0.0, base=H - 1,
                                 pattern=[[step, 2], [0, H]], channel_multiplier=-1).then_inc(center_set, 1)
                gp.wait_ge(center_set, 4 * n + 3)
                gp.affine_select(out=same_row, in_=same_row, compare_op=ALU.not_equal, fill=1.0 - 1.0 / H, base=0,
                                 pattern=[[-step, 2], [-1, H]], channel_multiplier=1).then_inc(center_set, 1)
            gp.affine_select(out=upto[:, 0:P], in_=upto[:, 0:P], compare_op=ALU.is_ge, fill=0.0, base=0,
                             pattern=[[1, P]], channel_multiplier=-1).then_inc(const_set, 1)

            def gather(t, source, dest):
                gp.wait_ge(idx_ready, t.number + 1)
                hold(gp)
                for u in range(U):
                    gp.indirect_dma_start(out=dest[:, t.slot, u], out_offset=None, in_=source,
                                          in_offset=bass.IndirectOffsetOnAxis(ap=slot_idx[:, t.slot, u:u + 1], axis=0))\
                        .then_inc(gathered[t.slot], 16)

            def add(t, dest):
                gp.wait_ge(put_idx_ready, t.number + 1)
                gp.wait_ge(put_ready, t.number + 1)
                hold(gp)
                for u in range(U):
                    gp.indirect_dma_start(out=dest, out_offset=bass.IndirectOffsetOnAxis(ap=put_idx[:, t.half, u:u + 1], axis=0),
                                          in_=put[:, t.half, u, :], in_offset=None, compute_op=ALU.add)\
                        .then_inc(added[t.half], 16)

            def landed(t):
                n = t.base // 2 + 1 if t.k is None else t.base // 2 + 1 + RING // 2 * t.k
                gp.wait_ge(added[t.half], 16 * U * n)
                gp.sem_inc(drained, 1)

            turns(gp, GROUPS, RING, lambda t: gather(t, x[:, :], got_x), lead=5)

            types = node_type.rearrange("(n a) -> n a", a=1)
            got_t = got_type[:, :, :].rearrange("p s (u a) -> p s u a", a=1)
            gather(Turn(B_AT, RING), types, got_t)
            for i in range(RING):
                n = (CHUNKS - i + RING - 1) // RING
                gp.wait_ge(rows_stored[i], 16 * n)
            gp.wait_ge(trash_zeroed, 16)

            def turn_b(t):
                add(t, table[:, :])
                if not (isinstance(t.number, int) and t.number == GROUPS - 1):
                    gather(t.ahead(B_AT + 1), types, got_t)
                landed(t)

            turns(gp, GROUPS, RING, turn_b, lead=4, tail=1)

            for n in range(RING - 1):
                gather(Turn(C_AT + n, RING), table[:, :], got)
            gp.wait_ge(sums_zeroed, 16 * (FULL_CHUNKS + 2))

            def turn_c(t):
                add(t.ahead(GROUPS), sums[:, :])
                if known(t, 0, GROUPS - (RING - 1)):
                    gather(t.ahead(C_AT + RING - 1), table[:, :], got)
                landed(t.ahead(GROUPS))

            turns(gp, GROUPS, RING, turn_c, lead=4, tail=5)
            gp.sem_inc(all_added, 1)

            def last_turn(t):
                n = parts(t.number)
                gp.wait_ge(t_inv_ready, t.number + 1)
                gp.tensor_tensor(t_s[0:n, t.slot, :, 0:H], t_s[0:n, t.slot, :, 0:H], wide(t_inv[0:n, t.slot], H), ALU.mult)\
                    .then_inc(t_agg, 1)
                gp.tensor_tensor(t_x[0:n, t.slot, :, 0:H], t_x[0:n, t.slot, :, 0:H], rows(beta_b[0:n], NR), ALU.add)\
                    .then_inc(t_xb, 1)

            turns(gp, CHUNKS, TRING, last_turn, lead=6, tail=1)

        @block.vector
        def _(dve):
            v = nc.vector
            st = Steps(dve, setup_step, 0)
            v.memset(attr_in[:, :, :, :], 0.0)
            st.add(v.memset(ew[:, FULL:TILES], 0.0))
            st.wait()
            dve.sem_inc(pads_set, 1)
            v.memset(half_pi[:, :], 3.141592653589793 / 2)
            v.memset(msg[:, :, :, :], 0.0)
            v.memset(attrT[:, :], 1.0)
            st.add(v.memset(hidden[:, :], 1.0))
            dve.wait_ge(order_loaded, 16 * 6)
            for n in range(RING):
                v.tensor_copy(slot_idx[:, n, :], order[:, U * n:U * (n + 1)]).then_inc(idx_ready, 1)
            dve.wait_ge(keys_loaded, 16 * 4)
            dve.wait_ge(const_set, 8)
            st.add(v.tensor_copy(keys[:, :], keys_i[:, :, :].rearrange("p n t -> p (n t)")))
            st.add(v.tensor_copy(trash[:, :], trash_i[:, :]))
            st.wait()
            st.add(v.tensor_tensor(rel[:, :].rearrange("p (g u) -> p g u", u=U), keys[:, :].rearrange("p (g u) -> p g u", u=U),
                                   rows(trash[:, :], 2 * GROUPS), ALU.subtract))
            dve.wait_ge(ew_loaded, 32)
            st.add(v.tensor_scalar(cw_t[:, :], ew[:, :], 0.5 / CUTOFF, ROUND, ALU.mult, ALU.add))
            st.wait()
            st.add(v.tensor_scalar(cw_t[:, :], cw_t[:, :], -ROUND, None, ALU.add))
            st.wait()
            st.add(v.scalar_tensor_tensor(out=cw_t[:, :], in0=ew[:, :], scalar=0.5 / CUTOFF, in1=cw_t[:, :],
                                          op0=ALU.mult, op1=ALU.subtract))
            st.wait()
            st.add(v.tensor_scalar(cutoff_w[:, :], cw_t[:, :], -1.0, None, ALU.mult))
            st.wait()
            v.tensor_tensor(cw_t[:, :], cw_t[:, :], cutoff_w[:, :], ALU.max).then_inc(cw_angle, 1)
            dve.wait_ge(cw_sin, 1)
            st.add(v.tensor_scalar(cw_t[:, :], cw_t[:, :], 0.5, 0.5, ALU.mult, ALU.add))
            st.add(v.tensor_scalar(cutoff_w[:, :], ew[:, :], CUTOFF, None, ALU.is_lt))
            st.wait()
            st.add(v.tensor_tensor(cutoff_w[:, :], cutoff_w[:, :], cw_t[:, :], ALU.mult))
            dve.wait_ge(w_turned, 3)
            v.tensor_copy(w1T[0:R, :], bank[4][0:R, 0:H])
            v.tensor_copy(w2T[0:H, :], bank[4][0:H, 64:64 + H])
            v.tensor_copy(embT[:, :], bank[4][0:DIM, 128:128 + KINDS]).then_inc(w_copied, 1)
            dve.wait_ge(w_turned, 4)
            v.tensor_copy(adapted[:, :], bank[5][0:DIM, 0:KINDS]).then_inc(w_copied, 1)
            dve.wait_ge(w_turned, 5)
            v.tensor_copy(logits[:, :], bank[6][0:KINDS, 0:KINDS]).then_inc(w_copied, 1)
            st.wait()
            dve.wait_ge(w_copied, 3)
            dve.wait_ge(center_set, 8)
            dve.wait_ge(weights_loaded, 16 * 8)
            v.tensor_tensor(center[:, 1].rearrange("q (b h) -> q b h", b=2), center[:, 0].rearrange("q (b h) -> q b h", b=2),
                            rows(gamma_b[0:PAIR], 2), ALU.mult).then_inc(center_set, 1)

            def next_idx(t):
                if known(t, 0, 3 * GROUPS - RING):
                    v.tensor_scalar(slot_idx[:, t.slot, :], order[:, bass.ds(U * (t.number + RING), U)], 0.0, None, ALU.add)\
                        .then_inc(idx_ready, 1)

            def arrived(t):
                dve.wait_ge(gathered[t.slot], 16 * U * (t.uses + 1))

            def row_stats(xg, d, st):
                st.add(v.tensor_reduce(s4[:, :], xg, AX.X, ALU.add))
                st.wait()
                st.add(v.tensor_scalar(m4[:, :], s4[:, :], 1.0 / H, None, ALU.mult))
                st.wait()
                st.add(v.tensor_tensor(d, xg, wide(m4[:, :], H), ALU.subtract))
                st.wait()
                st.add(v.tensor_tensor(sq4[:, :, :], d, d, ALU.mult))
                st.wait()
                st.add(v.tensor_reduce(v4[:, :], sq4[:, :, :], AX.X, ALU.add))
                st.wait()

            A_STEPS = 6

            def turn_a(t):
                if known(t, 0, GROUPS):
                    st = Steps(dve, a_step, A_STEPS * t.number)
                    arrived(t)
                    row_stats(got_x[:, t.slot], dev[:, t.slot], st)
                    next_idx(t)
                    v.tensor_scalar(group(dev0, t.number), dev[:, t.slot], 0.0, None, ALU.max)
                    st.add(v.tensor_scalar(group(var0, t.number), v4[:, :], 1.0 / H, EPS, ALU.mult, ALU.add))
                    assert st.n == A_STEPS
                if known(t, 1, GROUPS + 1):
                    dve.wait_ge(sig_ready, t.number)
                    v.tensor_tensor(hidden[0:H, :], ps_hid[0:H, :], sig[:, :], ALU.mult).then_inc(hidden_ready, 1)

            turns(dve, GROUPS + 1, RING, turn_a, lead=5, tail=1)
            dve.wait_ge(a_step, A_STEPS * GROUPS)
            v.sem_inc(var0_ready, 1)

            def take_keys(t):
                if not t.half_is_new:
                    dve.wait_ge(same_ready, t.number - 1)
                v.tensor_scalar(key4[:, t.half, :], group(keys, t.number), 0.0, None, ALU.add).then_inc(key4_ready, 1)

            def compare(t, st):
                dve.wait_ge(keys_turned, t.number + 1)
                if not t.half_is_new:
                    dve.wait_ge(summed, t.number - 1)
                for j in range(U):
                    last = v.scalar_tensor_tensor(out=same[:, t.half, SPAN_AT[j]:SPAN_AT[j] + SPAN[j]],
                                                  in0=ps_key[:, j * P:U * P], scalar=key4[:, t.half, j:j + 1],
                                                  in1=upto[:, 0:SPAN[j]], op0=ALU.is_equal, op1=ALU.mult,
                                                  accum_out=count[:, t.half, j:j + 1])
                last.then_inc(same_ready, 1)
                dve.wait_ge(same_ready, t.number + 1)
                st.add(v.tensor_scalar(last4[:, :], count[:, t.half], 1.0, None, ALU.is_equal))
                st.wait()
                st.add(v.tensor_tensor(off4[:, :], group(rel, t.number), last4[:, :], ALU.mult))
                if not t.half_is_new:
                    dve.wait_ge(drained, t.number - 1)
                st.wait()
                v.tensor_tensor(put_idx[:, t.half], off4[:, :], trash[:, :], ALU.add).then_inc(put_idx_ready, 1)

            take_keys(Turn(0, RING))
            dve.wait_ge(sd0_ready, 1)
            b0 = Steps(dve, b_step, 0)
            b0.add(v.reciprocal(rw[:, :], var0[:, :]))
            b0.wait()
            b0.add(v.tensor_tensor(rw[:, :], rw[:, :], ew[:, :], ALU.mult))
            compare(Turn(0, RING), b0)
            b0.wait()

            B_FIRST = b0.n
            B_STEPS = 3

            def turn_b(t):
                g = t.number
                st = Steps(dve, b_step, B_FIRST + B_STEPS * g)
                take_keys(t.ahead(1))
                if not t.half_is_new:
                    dve.wait_ge(summed, g - 1)
                v.tensor_tensor(msg[:, t.half, :, 0:H], group(dev0, g), wide(group(rw, g), H), ALU.mult).then_inc(msg_ready, 1)
                compare(t.ahead(1), st)
                m = t.ahead(B_AT)
                arrived(m)
                st.add(v.tensor_scalar(group(type_src, g), got_type[:, m.slot], 0.0, None, ALU.add))
                st.wait()
                next_idx(m)
                assert st.n == B_STEPS

            turns(dve, GROUPS, RING, turn_b, lead=5)
            dve.wait_ge(b_step, B_FIRST + B_STEPS * GROUPS)
            dve.wait_ge(gate_copied, GROUPS)

            def take_types(t):
                v.tensor_scalar(type4[:, :], group(type_src, t.number), 0.0, None, ALU.add).then_inc(type4_ready, 1)

            def one_hot(t):
                dve.wait_ge(types_turned, t.number + 1)
                if known(t, 1, GROUPS):
                    dve.wait_ge(logit_done, t.number)
                v.tensor_scalar(onehot[:, :], ps_type[0:KINDS, :], kind_col[0:KINDS, 0:1], None, ALU.is_equal)\
                    .then_inc(onehot_ready, 1)

            def node_var(t, st):
                n = parts(t.number)
                dve.wait_ge(c_squared, 2 * t.number + 2)
                st.add(v.tensor_reduce(c_v[0:n, :], c_q[0:n], AX.X, ALU.add))
                st.wait()
                v.tensor_scalar(c_v[0:n, :], c_v[0:n, :], 1.0 / H, EPS, ALU.mult, ALU.add).then_inc(c_var, 1)

            def node_h(t, st):
                n = parts(t.number)
                dve.wait_ge(c_std, t.number + 1)
                st.add(v.reciprocal(c_r[0:n, :], c_sd[0:n, :]))
                if known(t, 2, CHUNKS):
                    uses = t.base // 2 if t.k is None else t.base // 2 + RING // 2 * t.k
                    dve.wait_ge(c_stored[t.half], 16 * uses)
                st.wait()
                for i in range(2):
                    last = v.scalar_tensor_tensor(out=c_h[0:n, t.half, i * HALF:(i + 1) * HALF],
                                                  in0=ps_dev[i][0:n, 0:HALF * H].rearrange("p (r h) -> p r h", h=H), scalar=0.0,
                                                  in1=wide(c_r[0:n, i * HALF:(i + 1) * HALF], H), op0=ALU.max, op1=ALU.mult)
                last.then_inc(c_h_ready, 1)

            take_types(Turn(0, RING))
            one_hot(Turn(0, RING))
            C_EDGE, C_NODE = 12, 2

            def turn_c(t):
                g = t.number
                if t.k is None:
                    first = C_EDGE * min(g, GROUPS) + 2 * min(g, GROUPS - 1) + C_NODE * max(g - 1, 0)
                else:
                    first = (C_EDGE + 2 + C_NODE) * g - C_NODE
                st = Steps(dve, c_step, first)
                m, n = t.ahead(C_AT), t.ahead(GROUPS)
                if known(t, 0, GROUPS - 1):
                    take_types(t.ahead(1))
                    take_keys(n.ahead(1))
                if known(t, 0, GROUPS):
                    rowsg = got[:, m.slot]
                    arrived(m)
                    row_stats(got[:, m.slot, :, 0:H], dev[:, m.slot], st)
                    v.tensor_scalar(ve4[:, m.slot], v4[:, :], 1.0 / H, EPS, ALU.mult, ALU.add).then_inc(var_ready, 1)
                    dve.wait_ge(logit_done, g + 1)
                    for u in range(U):
                        last = v.scalar_tensor_tensor(out=hit[:, u, :], in0=kind_row[:, :], scalar=rowsg[:, u, H + 1:H + 2],
                                                      in1=ps_logit[:, u * KINDS:(u + 1) * KINDS], op0=ALU.is_equal,
                                                      op1=ALU.mult, accum_out=lg4[:, u:u + 1])
                    last.then_inc(logit_read, 1)
                    dve.wait_ge(sd_ready, g + 1)
                    st.add(v.reciprocal(cf4[:, :], sd4[:, m.slot]))
                    st.wait()
                    st.add(v.tensor_tensor(cf4[:, :], cf4[:, :], group(cutoff_w, g), ALU.mult))
                    st.wait()
                    st.add(v.tensor_tensor(cf4[:, :], cf4[:, :], rowsg[:, :, H], ALU.mult))
                    dve.wait_ge(logit_read, g + 1)
                    st.add(v.tensor_tensor(gl4[:, :, :], group(gate, g), wide(lg4[:, :], H), ALU.add))
                    dve.wait_ge(summed, GROUPS + g - 1)
                    st.add(v.tensor_scalar(msg[:, n.half, :, H], rowsg[:, :, H], 0.0, None, ALU.add))
                    st.wait()
                    st.add(v.scalar_tensor_tensor(out=dev[:, m.slot], in0=dev[:, m.slot], scalar=0.0, in1=wide(cf4[:, :], H),
                                                  op0=ALU.max, op1=ALU.mult))
                    st.wait()
                    st.add(v.tensor_tensor(msg[:, n.half, :, 0:H], gl4[:, :, :], dev[:, m.slot], ALU.mult))
                    st.wait()
                    v.sem_inc(msg_ready, 1)
                    next_idx(m)
                    assert st.n == C_EDGE, st.n
                if known(t, 1, CHUNKS + 1):
                    node_var(t.ahead(-1), st)
                if known(t, 0, GROUPS - 1):
                    one_hot(t.ahead(1))
                    compare(n.ahead(1), st)
                if known(t, 1, CHUNKS + 1):
                    node_h(t.ahead(-1), st)

            turns(dve, GROUPS + 1, RING, turn_c, lead=5, tail=5)

            def inv_tot(t, st):
                n = parts(t.number)
                dve.wait_ge(t_loaded[t.slot], 48 * (t.uses + 1))
                st.add(v.tensor_scalar(t_inv[0:n, t.slot], t_s[0:n, t.slot, :, H], 1e-8, None, ALU.max))
                st.wait()
                v.reciprocal(t_inv[0:n, t.slot], t_inv[0:n, t.slot]).then_inc(t_inv_ready, 1)

            def last_turn(t):
                if t.k is None:
                    first = min(t.number, CHUNKS - 1) + 3 * min(max(t.number - 2, 0), CHUNKS) + 1
                else:
                    first = 4 * t.number - 5
                st = Steps(dve, t_step, first)
                a = t.ahead(-2)
                n = parts(a.number)
                if known(a, 0, CHUNKS):
                    dve.wait_ge(t_split, 2 * a.number + 2)
                    st.add(v.tensor_reduce(t_v[0:n, a.slot], t_h[0:n, a.slot], AX.X, ALU.add))
                    st.wait()
                    v.tensor_scalar(t_v[0:n, a.slot], t_v[0:n, a.slot], 1.0 / H, EPS, ALU.mult, ALU.add).then_inc(t_var, 1)
                if known(t, 0, CHUNKS - 1):
                    inv_tot(t.ahead(1), st)
                if known(t, 0, CHUNKS):
                    c = parts(t.number)
                    dve.wait_ge(t_agg, t.number + 1)
                    v.tensor_tensor(t_h[0:c, t.slot], t_h[0:c, t.slot], t_s[0:c, t.slot, :, 0:H], ALU.add).then_inc(t_x2, 1)
                if known(a, 0, CHUNKS):
                    y = t_s[0:n, a.slot, :, 0:H]
                    dve.wait_ge(t_std, a.number + 1)
                    st.add(v.reciprocal(t_sd[0:n, a.slot], t_sd[0:n, a.slot]))
                    st.wait()
                    st.add(v.tensor_tensor(y, y, wide(t_sd[0:n, a.slot], H), ALU.mult))
                    st.wait()
                    dve.wait_ge(t_xb, a.number + 1)
                    v.tensor_tensor(t_h[0:n, a.slot], y, t_x[0:n, a.slot, :, 0:H], ALU.add).then_inc(t_out, 1)

            inv_tot(Turn(0, TRING), Steps(dve, t_step, 0))
            turns(dve, CHUNKS + 2, TRING, last_turn, lead=9, tail=6)

        @block.scalar
        def _(act):
            s = nc.scalar
            act.wait_ge(cw_angle, 1)
            s.activation(cw_t[:, :], cw_t[:, :], ACT.Sin, bias=half_pi[:, 0:1], scale=-2 * 3.141592653589793)\
                .then_inc(cw_sin, 1)
            act.wait_ge(nodes_loaded, 64)

            def turn_a(t):
                g = t.number
                if known(t, 0, GROUPS):
                    act.wait_ge(attr_turned, g + 1)
                    if known(t, 1, GROUPS):
                        act.wait_ge(hid_done, g)
                    s.copy(attrT[0:R, :], ps_attr[0:R, :]).then_inc(attrT_ready, 1)
                    n = parts(g)
                    act.wait_ge(x_loaded[t.slot], 16 * (t.uses + 1))
                    if not t.slot_is_new:
                        act.wait_ge(rows_stored[t.slot], 16 * t.uses)
                    hold(act)
                    at = bass.ds(g, 1)
                    s.copy(rows_out[0:n, t.slot, :, 0:H], x_in[0:n, t.slot])
                    s.copy(rows_out[0:n, t.slot, :, H], vec_in[0:n, at, :].rearrange("p a r -> p (a r)"))
                    s.copy(rows_out[0:n, t.slot, :, H + 1], type_in[0:n, at, :].rearrange("p a r -> p (a r)")).then_inc(rows_built, 1)
                if known(t, 1, GROUPS + 1):
                    act.wait_ge(gate_done, g)
                    hold(act)
                    s.copy(group(gate, g - 1), ps_gate[:, 0:U * H].rearrange("p (u h) -> p u h", u=U)).then_inc(gate_copied, 1)
                if known(t, 0, GROUPS):
                    act.wait_ge(hid_done, g + 1)
                    if known(t, 1, GROUPS):
                        act.wait_ge(hidden_ready, g)
                    s.activation(sig[:, :], ps_hid[0:H, :], ACT.Sigmoid).then_inc(sig_ready, 1)

            act.wait_ge(setup_step, 2)
            turns(act, GROUPS + 1, RING, turn_a, lead=5, tail=5)
            act.wait_ge(var0_ready, 1)
            s.activation(var0[:, :], var0[:, :], ACT.Sqrt).then_inc(sd0_ready, 1)

            def copy_sums(t):
                act.wait_ge(summed, t.number + 1)
                if not t.half_is_new:
                    act.wait_ge(drained, t.number - 1)
                s.copy(put[:, t.half].rearrange("p u w -> p (u w)"), ps_sum[:, 0:U * W])\
                    .then_inc(put_ready, 1)

            turns(act, GROUPS, RING, copy_sums, lead=5)

            def square_c(t):
                n = parts(t.number)
                for i in range(2):
                    act.wait_ge(c_centered, 2 * t.number + i + 1)
                    if i == 0 and known(t, 1, CHUNKS):
                        act.wait_ge(c_var, t.number)
                    s.activation(c_q[0:n, i * HALF:(i + 1) * HALF].rearrange("p r h -> p (r h)"),
                                 ps_dev[i][0:n, 0:HALF * H], ACT.Square).then_inc(c_squared, 1)

            def turn_c(t):
                g = t.number
                m = t.ahead(C_AT)
                if known(t, 1, CHUNKS + 1):
                    square_c(t.ahead(-1))
                if known(t, 0, CHUNKS):
                    for i in range(2):
                        act.wait_ge(c_turned, 2 * g + i + 1)
                        s.copy(xT[:, i, :], ps_turn[i][0:W + H, :]).then_inc(c_copied, 1)
                if known(t, 0, GROUPS):
                    act.wait_ge(var_ready, g + 1)
                    s.activation(sd4[:, m.slot], ve4[:, m.slot], ACT.Sqrt).then_inc(sd_ready, 1)
                    copy_sums(t.ahead(GROUPS))
                if known(t, 1, CHUNKS + 1):
                    n = parts(t.ahead(-1).number)
                    act.wait_ge(c_var, g)
                    s.activation(c_sd[0:n, :], c_v[0:n, :], ACT.Sqrt).then_inc(c_std, 1)

            turns(act, GROUPS + 1, RING, turn_c, lead=4, tail=2)

            def last_turn(t):
                a = t.ahead(-2)
                if known(a, 0, CHUNKS):
                    n = parts(a.number)
                    act.wait_ge(t_var, a.number + 1)
                    s.activation(t_sd[0:n, a.slot], t_v[0:n, a.slot], ACT.Sqrt).then_inc(t_std, 1)
                if known(t, 0, CHUNKS):
                    n = parts(t.number)
                    for i in range(2):
                        act.wait_ge(t_turned, 2 * t.number + i + 1)
                        s.copy(xT[0:PAIR, i, :], t_turn[i][0:PAIR, :]).then_inc(t_copied, 1)
                    for i in range(2):
                        act.wait_ge(t_centered, 2 * t.number + i + 1)
                        both = t_dev[(2 * t.base + i) % 3][0:n]
                        at = slice(i * HALF, (i + 1) * HALF)
                        s.activation(t_h[0:n, t.slot, at].rearrange("p (b i k) h -> p b i (k h)", b=2, i=2), both[:, :, :, 0, :],
                                     ACT.Square)
                        for b in range(2):
                            last = s.copy(t_s[0:n, t.slot, i * HALF + 4 * b:i * HALF + 4 * b + 4, 0:H]
                                          .rearrange("p (i k) h -> p i k h", i=2),
                                          both[:, b, :, 1, :].rearrange("p i (k h) -> p i k h", k=2))
                        last.then_inc(t_split, 1)

            turns(act, CHUNKS + 2, TRING, last_turn, lead=6, tail=3)

        @block.tensor
        def _(pe):
            te = nc.tensor
            pe.wait_ge(const_set, 8)
            pe.wait_ge(weights_loaded, 16 * 8)
            te.transpose(bank[4][0:R, 0:H], w1_in[:, :], ident[0:H, 0:H]).then_inc(w_turned, 1)
            te.transpose(bank[4][0:H, 64:64 + H], w2_in[:, :], ident[0:H, 0:H]).then_inc(w_turned, 1)
            te.transpose(bank[4][0:DIM, 128:128 + KINDS], emb_in[:, :], ident[0:KINDS, 0:KINDS]).then_inc(w_turned, 1)
            pe.wait_ge(w_copied, 1)
            te.matmul(bank[5][0:DIM, 0:KINDS], adapt_in[:, :], embT[:, :], start=True, stop=True).then_inc(w_turned, 1)
            pe.wait_ge(w_copied, 2)
            te.matmul(bank[6][0:KINDS, 0:KINDS], adapted[:, :], embT[:, :], start=True, stop=True).then_inc(w_turned, 1)
            pe.wait_ge(w_copied, 3)

            def turn_keys(t):
                pe.wait_ge(key4_ready, t.number + 1)
                if known(t, 1, 2 * GROUPS):
                    pe.wait_ge(same_ready, t.number)
                hold(pe)
                for u in range(U):
                    last = te.transpose(ps_key[:, u * P:(u + 1) * P], key4[:, t.half, u:u + 1].broadcast_to([P, P]), ident[:, :])
                last.then_inc(keys_turned, 1)

            def sum_equal(t):
                pe.wait_ge(same_ready, t.number + 1)
                pe.wait_ge(msg_ready, t.number + 1)
                if known(t, 1, 2 * GROUPS):
                    pe.wait_ge(put_ready, t.number)
                hold(pe)
                for i in range(U):
                    for j in range(i + 1):
                        at = SPAN_AT[j] + (i - j) * P
                        last = te.matmul(ps_sum[:, i * W:(i + 1) * W], same[:, t.half, at:at + P], msg[:, t.half, j],
                                         start=(j == 0), stop=(j == i))
                last.then_inc(summed, 1)

            def turn_a(t):
                g = t.number
                if known(t, 0, GROUPS):
                    loads = 2 if isinstance(g, int) and g == GROUPS - 1 else 1
                    pe.wait_ge(attr_loaded[t.slot], 16 * (t.uses + loads))
                    if known(t, 1, GROUPS):
                        pe.wait_ge(attrT_ready, g)
                    hold(pe)
                    for u in range(U):
                        last = te.transpose(ps_attr[0:R, u * P:(u + 1) * P], attr_in[:, t.slot, u, :], ident[:, :])
                    last.then_inc(attr_turned, 1)
                if known(t, 1, GROUPS + 1):
                    pe.wait_ge(hidden_ready, g)
                    if known(t, 2, GROUPS + 1):
                        pe.wait_ge(gate_copied, g - 1)
                    hold(pe)
                    for u in range(U):
                        last = te.matmul(ps_gate[:, u * H:(u + 1) * H], hidden[0:H + 1, u * P:(u + 1) * P], w2T[:, :],
                                         start=True, stop=True)
                    last.then_inc(gate_done, 1)
                if known(t, 0, GROUPS):
                    pe.wait_ge(attrT_ready, g + 1)
                    hold(pe)
                    te.matmul(ps_hid[0:H, :], w1T[:, :], attrT[0:R + 1, :], start=True, stop=True).then_inc(hid_done, 1)

            turns(pe, GROUPS + 1, RING, turn_a, lead=5, tail=5)

            turn_keys(Turn(0, RING))

            def turn_b(t):
                turn_keys(t.ahead(1))
                sum_equal(t)

            turns(pe, GROUPS, RING, turn_b, lead=5)

            def turn_types(t):
                pe.wait_ge(type4_ready, t.number + 1)
                if known(t, 1, GROUPS):
                    pe.wait_ge(onehot_ready, t.number)
                hold(pe)
                for u in range(U):
                    last = te.transpose(ps_type[:, u * P:(u + 1) * P], type4[:, u:u + 1].broadcast_to([P, P]), ident[:, :])
                last.then_inc(types_turned, 1)

            def edge_logits(t):
                pe.wait_ge(onehot_ready, t.number + 1)
                if known(t, 1, GROUPS):
                    pe.wait_ge(logit_read, t.number)
                hold(pe)
                for u in range(U):
                    last = te.matmul(ps_logit[:, u * KINDS:(u + 1) * KINDS], onehot[:, u * P:(u + 1) * P], logits[:, :],
                                     start=True, stop=True)
                last.then_inc(logit_done, 1)

            pe.wait_ge(gate_copied, GROUPS)
            turn_types(Turn(0, RING))
            edge_logits(Turn(0, RING))
            pe.wait_ge(center_set, 9)

            def turn_c(t):
                g = t.number
                n = parts(g)
                more = known(t, 0, GROUPS - 1)
                if more:
                    turn_keys(t.ahead(GROUPS + 1))
                    turn_types(t.ahead(1))
                loads = t.base // 2 + 1 if t.k is None else t.base // 2 + 1 + RING // 2 * t.k
                pe.wait_ge(c_loaded[t.half], 16 * loads)
                for i in range(2):
                    if known(t, 1, CHUNKS):
                        pe.wait_ge(c_copied, 2 * (g - 1) + i + 1)
                    hold(pe)
                    for b in range(BLOCKS):
                        r = i * HALF + 2 * b
                        last = te.transpose(ps_turn[i][0:W + H, b * P:b * P + n],
                                            c_x[0:n, t.half].rearrange("p r w -> p (r w)")[:, r * W:r * W + W + H], ident[0:n, 0:n])
                    last.then_inc(c_turned, 1)
                sum_equal(t.ahead(GROUPS))
                if more:
                    edge_logits(t.ahead(1))
                for i in range(2):
                    pe.wait_ge(c_copied, 2 * g + i + 1)
                    if i == 0 and known(t, 1, CHUNKS):
                        pe.wait_ge(c_h_ready, g)
                    hold(pe)
                    for b in range(BLOCKS):
                        last = te.matmul(ps_dev[i][0:n, b * PAIR:(b + 1) * PAIR], xT[:, i, b * P:b * P + n], center_w[:, :],
                                         start=True, stop=True)
                    last.then_inc(c_centered, 1)

            turns(pe, GROUPS, RING, turn_c, lead=4, tail=1)
            pe.wait_ge(c_h_ready, CHUNKS)

            def last_turn(t):
                g = t.number
                n = parts(g)
                pe.wait_ge(t_x2, g + 1)
                for i in range(2):
                    if known(t, 1, CHUNKS):
                        pe.wait_ge(t_copied, 2 * (g - 1) + i + 1)
                    hold(pe)
                    for b in range(BLOCKS):
                        r = i * HALF + 2 * b
                        last = te.transpose(t_turn[i][0:PAIR, b * P:b * P + n],
                                            t_h[0:n, t.slot, r:r + 2].rearrange("p r h -> p (r h)"), ident[0:n, 0:n])
                    last.then_inc(t_turned, 1)
                for i in range(2):
                    pe.wait_ge(t_copied, 2 * g + i + 1)
                    if known(t, 2, CHUNKS):
                        pe.wait_ge(t_split, 2 * g + i - 2)
                    hold(pe)
                    both = t_dev[(2 * t.base + i) % 3]
                    for b in range(BLOCKS):
                        last = te.matmul(both[0:n, b // 2, b % 2].rearrange("p k f -> p (k f)"), xT[0:PAIR, i, b * P:b * P + n],
                                         center[:, :].rearrange("q k f -> q (k f)"), start=True, stop=True)
                    last.then_inc(t_centered, 1)

            turns(pe, CHUNKS, TRING, last_turn, lead=6, tail=1)


_INS = ['x', 'src', 'dst', 'edge_attr_40', 'edge_weight', 'node_type_119', 'node_vec', 'L1_gnn_W1', 'L1_gnn_b1',
        'L1_gnn_W2', 'L1_gnn_b2', 'L1_gnn_emb', 'L1_gnn_adaptW', 'L1_gnn_gamma', 'L1_gnn_beta']


def kernel(**inputs):
    import numpy as _np
    import concourse.bacc as _bacc
    from concourse import mybir as _mybir
    from concourse.bass_utils import run_bass_kernel_spmd as _run

    nc = _bacc.Bacc("TRN2", target_bir_lowering=False, num_devices=1)
    arrays, args = {}, []
    for name in _INS:
        a = _np.ascontiguousarray(inputs[name])
        arrays[f"in_{name}_dram"] = a
        args.append(nc.dram_tensor(f"in_{name}_dram", a.shape, _mybir.dt.from_np(a.dtype), kind="ExternalInput").ap())
    shape = inputs['x'].shape
    args.append(nc.dram_tensor("out_0_dram", shape, _mybir.dt.from_np(_np.dtype('float32')), kind="ExternalOutput").ap())
    gnn_kernel(nc, *args)
    r = _run(nc, [arrays], core_ids=[0])
    return r.results[0]["out_0_dram"]
```

```python
import concourse.bass as bass
from concourse import mybir
from contextlib import ExitStack


class Turn:

    def __init__(self, base, ring, k=None):
        self.base, self.ring, self.k = base, ring, k

    @property
    def number(self):
        return self.base if self.k is None else self.base + self.ring * self.k

    @property
    def slot(self):
        return self.base % self.ring

    @property
    def uses(self):
        return self.base // self.ring if self.k is None else self.base // self.ring + self.k

    @property
    def half(self):
        return self.base % 2

    @property
    def half_is_new(self):
        return self.k is None and self.base < 2

    def ahead(self, turns):
        return Turn(self.base + turns, self.ring, self.k)

    @property
    def slot_is_new(self):
        return self.k is None and self.base < self.ring


def turns(eng, count, ring, body, lead, tail=0):
    rounds, rest = divmod(count - lead - tail, ring)
    assert rest == 0 and lead >= ring
    for n in range(lead):
        body(Turn(n, ring))
    with eng.Fori(0, rounds) as k:
        for r in range(ring):
            body(Turn(lead + r, ring, k))
    for n in range(count - tail, count):
        body(Turn(n, ring))


def known(t, least, most):
    return t.k is not None or least <= t.base < most


class Steps:

    def __init__(self, eng, sem, first):
        self.eng, self.sem, self.first, self.n = eng, sem, first, 0

    def add(self, instruction):
        instruction.then_inc(self.sem, 1)
        self.n += 1
        return self.n

    def wait(self, step=None):
        self.eng.wait_ge(self.sem, self.first + (step or self.n))


def gnn_kernel(nc, x, src, dst, edge_attr, edge_weight, node_type, node_vec, W1, b1, W2, b2, emb, adaptW, gamma,
               beta, out):
    fp32 = mybir.dt.float32
    i32 = mybir.dt.int32
    fp16 = mybir.dt.float16
    bf16 = mybir.dt.bfloat16
    ALU = mybir.AluOpType
    ACT = mybir.ActivationFunctionType
    AX = mybir.AxisListType

    P = 128
    N, H = x.shape
    E, R = edge_attr.shape
    KINDS, DIM = emb.shape
    EPS = 1e-5
    CUTOFF = 6.0
    ROUND = 1.5 * 2.0 ** 23
    BASE = 1024

    FULL = E // P
    REM = E - P * FULL
    TILES = FULL + 1
    U = 4
    GROUPS = TILES // U
    assert GROUPS * U == TILES
    RING = 4
    W = H + 2
    TYPE_P = 125
    TYPE_COLS = N // TYPE_P
    assert TYPE_P * TYPE_COLS == N
    PACK, PACK_BASE = 3, 128
    LOOK = -(-TYPE_COLS // PACK)
    assert KINDS <= PACK_BASE
    TRASH = N
    ROWS = N + U * P
    SPAN = [(U - j) * P for j in range(U)]
    SPAN_AT = [sum(SPAN[:j]) for j in range(U)]

    NR = 16
    CHUNK = P * NR
    FULL_CHUNKS = N // CHUNK
    LAST_P = (N - FULL_CHUNKS * CHUNK) // NR
    CHUNKS = FULL_CHUNKS + 1
    assert FULL_CHUNKS * CHUNK + LAST_P * NR == N
    TRING = 9
    LAG = 7
    EARLY = TRING, 6
    HALF = NR // 2
    PAIR = 2 * H
    BLOCKS = HALF // 2

    table = nc.dram_tensor("node_table", (ROWS, W), fp32, kind="Internal").ap()
    sums = nc.dram_tensor("edge_sums", (ROWS, W), fp32, kind="Internal").ap()
    hs = nc.dram_tensor("hidden_nodes", (N, H), fp32, kind="Internal").ap()

    def chunk(t, c):
        if isinstance(c, int) and c == FULL_CHUNKS:
            return t[FULL_CHUNKS * CHUNK:N].rearrange("(p r) f -> p (r f)", r=NR)
        v = t[0:FULL_CHUNKS * CHUNK].rearrange("(c p r) f -> c p (r f)", p=P, r=NR)
        return v[bass.ds(c, 1)].rearrange("a p f -> (a p) f")

    def parts(c):
        return LAST_P if isinstance(c, int) and c == FULL_CHUNKS else P

    ctx = ExitStack()
    with ctx:
        def sb(name, shape, dt=fp32):
            return ctx.enter_context(nc.sbuf_tensor(name, shape, dt))

        def sem(name):
            return ctx.enter_context(nc.semaphore(name))

        order = sb("order", [P, 2 * TILES], i32)
        keys_i = sb("keys_i", [P, 2, TILES], i32)
        keys = sb("keys", [P, 2 * TILES])
        rel = sb("rel", [P, 2 * TILES])
        digits = sb("digits", [P, 2, 2 * TILES], fp16)
        digit_t = sb("digit_t", [P, 2 * TILES])
        trash_i = sb("trash_i", [P, U], i32)
        trash = sb("trash", [P, U])
        ew = sb("ew", [P, TILES])
        cutoff_w = sb("cutoff_w", [P, TILES])
        cw_t = sb("cw_t", [P, TILES])
        half_pi = sb("half_pi", [P, 1])
        early = sb("early", [P, TILES * H + RING * NR * (H + W)])
        dev0 = early[:, 0:TILES * H].rearrange("p (t h) -> p t h", h=H)
        gate = sb("gate", [P, TILES, H])
        var0 = sb("var0", [P, TILES])
        rw = sb("rw", [P, TILES])
        type_src = sb("type_src", [P, TILES])
        src_part = sb("src_part", [P, TILES])
        src_digit = sb("src_digit", [P, TILES])
        src_col = sb("src_col", [P, TILES])
        packed = sb("packed", [P, TILES])
        digit_of = sb("digit_of", [P, PACK, TILES])
        ident = sb("ident", [P, P])
        ident16 = sb("ident16", [P, 2, P], fp16)
        eps = sb("eps", [P, 1])
        upto = sb("upto", [P, U * P])
        kind_row = sb("kind_row", [P, LOOK])
        kind_col = sb("kind_col", [P, 1])
        zeros = sb("zeros", [P, NR * W])
        gamma_b = sb("gamma_b", [P, H])
        beta_b = sb("beta_b", [P, H])
        w1_in = sb("w1_in", [H, R])
        w2_in = sb("w2_in", [H, H])
        emb_in = sb("emb_in", [KINDS, DIM])
        adapt_in = sb("adapt_in", [DIM, DIM])
        w1T = sb("w1T", [R + 1, H])
        w2T = sb("w2T", [H + 1, H])
        embT = sb("embT", [DIM, KINDS])
        adapted = sb("adapted", [DIM, KINDS])
        logits = sb("logits", [KINDS, 3, KINDS], bf16)
        logit_t = sb("logit_t", [KINDS, 2, KINDS])
        type_rows = sb("type_rows", [TYPE_P, TYPE_COLS], i32)
        type_table = sb("type_table", [TYPE_P, PACK, LOOK], bf16)
        vec_in = sb("vec_in", [P, CHUNKS, NR])
        type_in = sb("type_in", [P, CHUNKS, NR], i32)
        at = TILES * H
        x_in = early[:, at:at + RING * NR * H].rearrange("p (s r h) -> p s r h", s=RING, h=H)
        at += RING * NR * H
        rows_out = early[:, at:at + RING * NR * W].rearrange("p (s r w) -> p s r w", s=RING, w=W)
        slot_idx = sb("slot_idx", [P, RING, U], i32)
        got = sb("got", [P, RING, U, W])
        got_x = sb("got_x", [P, RING, U, H])
        s4 = sb("s4", [P, U])
        v4 = sb("v4", [P, U])
        cm4 = sb("cm4", [P, U])
        sq4 = sb("sq4", [P, U, H])
        dev = sb("dev", [P, RING, U, H])
        sd4 = sb("sd4", [P, RING, U])
        lg4 = sb("lg4", [P, U])
        cf4 = sb("cf4", [P, U])
        gl4 = sb("gl4", [P, U, H])
        hit = sb("hit", [P, U, KINDS])
        key4 = sb("key4", [P, 2, U])
        digit4 = sb("digit4", [P, 2, 2, U], fp16)
        type4 = sb("type4", [P, U], fp16)
        off_row = sb("off_row", [P, U * P])
        onehot = sb("onehot", [P, U * P], bf16)
        look_hit = sb("look_hit", [P, U, LOOK], bf16)
        col4 = sb("col4", [P, U])
        found4 = sb("found4", [P, U])
        msg = sb("msg", [P, U, W])
        left = sb("left", [P, U, W])
        msg_parts = sb("msg_parts", [P, 2, 3, U, W], bf16)
        same = sb("same", [P, 2, sum(SPAN)], bf16)
        count = sb("count", [P, 2, U])
        off4 = sb("off4", [P, U])
        put_idx = sb("put_idx", [P, 2, U], i32)
        put = sb("put", [P, 2, U, W])
        attr_in = sb("attr_in", [P, RING, U, R])
        attrT = sb("attrT", [64, U * P])
        sig = sb("sig", [H, U * P])
        hidden = sb("hidden", [64, U * P])
        center = sb("center", [PAIR, 2, PAIR])
        center_w = sb("center_w", [W + H, PAIR])
        c_x = sb("c_x", [P, 2, NR, W])
        c_q = sb("c_q", [P, NR, H])
        c_h = sb("c_h", [P, 2, NR, H])
        c_v = sb("c_v", [P, NR])
        c_sd = sb("c_sd", [P, NR])
        c_r = sb("c_r", [P, NR])
        xT = sb("xT", [W + H, 2, BLOCKS * P])
        assert TRING * NR * (2 * W) <= TILES * H + RING * NR * (H + W) and TRING * NR * H <= TILES * H
        at = TRING * NR * W
        t_x = early[:, 0:at].rearrange("p (s r w) -> p s r w", s=TRING, w=W)
        t_s = early[:, at:2 * at].rearrange("p (s r w) -> p s r w", s=TRING, w=W)
        t_h = gate[:, 0:TRING * NR, :].rearrange("p (s r) h -> p s r h", s=TRING)
        t_inv = sb("t_inv", [P, TRING, NR])
        t_v = sb("t_v", [P, TRING, NR])
        t_sd = sb("t_sd", [P, TRING, NR])

        ps = ctx.enter_context(nc.psum_tensor("ps", [P, 8, 512], fp32))
        bank = [ps[:, i, :] for i in range(8)]
        ps_attr, ps_hid, ps_gate, ps_key, ps_sum, ps_type = bank[0:6]
        ps_logit = bank[0]
        ps_look = [bank[i] for i in (0, 1, 2, 7)]
        ps_turn = [bank[1], bank[2]]
        ps_dev = [bank[6], bank[7]]
        t_turn = [bank[0], bank[1]]
        assert 2 * TRING % 3 == 0
        t_dev = [ps[:, 2 * i + 2:2 * i + 4, 0:2 * 2 * PAIR].rearrange("p b (i k f) -> p b i k f", i=2, k=2) for i in range(3)]

        keys_loaded = sem("keys_loaded")
        order_loaded = sem("order_loaded")
        ew_loaded = sem("ew_loaded")
        nodes_loaded = sem("nodes_loaded")
        weights_loaded = sem("weights_loaded")
        pads_set = sem("pads_set")
        const_set = sem("const_set")
        w_turned = sem("w_turned")
        w_copied = sem("w_copied")
        cw_angle = sem("cw_angle")
        cw_sin = sem("cw_sin")
        setup_step = sem("setup_step")
        types_loaded = sem("types_loaded")
        table_packed = sem("table_packed")
        looked = sem("looked")
        found = sem("found")
        unpack_step = sem("unpack_step")
        x_loaded = [sem(f"x_loaded{i}") for i in range(RING)]
        rows_built = sem("rows_built")
        rows_stored = [sem(f"rows_stored{i}") for i in range(RING)]
        type_read = sem("type_read")
        trash_zeroed = sem("trash_zeroed")
        sums_zeroed = sem("sums_zeroed")
        idx_ready = sem("idx_ready")
        gathered = [sem(f"gathered{i}") for i in range(RING)]
        a_step = sem("a_step")
        var0_ready = sem("var0_ready")
        sd0_ready = sem("sd0_ready")
        b_step = sem("b_step")
        c_step = sem("c_step")
        key4_ready = sem("key4_ready")
        keys_turned = sem("keys_turned")
        same_ready = sem("same_ready")
        put_idx_ready = sem("put_idx_ready")
        summed = sem("summed")
        put_ready = sem("put_ready")
        added = [sem(f"added{i}") for i in range(RING)]
        drained = sem("drained")
        attr_loaded = [sem(f"attr_loaded{i}") for i in range(RING)]
        attr_turned = sem("attr_turned")
        attrT_ready = sem("attrT_ready")
        hid_done = sem("hid_done")
        sig_ready = sem("sig_ready")
        hidden_ready = sem("hidden_ready")
        gate_done = sem("gate_done")
        gate_copied = sem("gate_copied")
        var_ready = sem("var_ready")
        sd_ready = sem("sd_ready")
        type4_ready = sem("type4_ready")
        types_turned = sem("types_turned")
        onehot_ready = sem("onehot_ready")
        logit_done = sem("logit_done")
        logit_read = sem("logit_read")
        msg_ready = sem("msg_ready")
        msg_made = sem("msg_made")
        hi_made = sem("hi_made")
        left_made = sem("left_made")
        mid_made = sem("mid_made")
        dev_ready = sem("dev_ready")
        sq_ready = sem("sq_ready")
        logit_split = sem("logit_split")
        center_set = sem("center_set")
        c_loaded = [sem(f"c_loaded{i}") for i in range(2)]
        c_turned = sem("c_turned")
        c_copied = sem("c_copied")
        c_centered = sem("c_centered")
        c_squared = sem("c_squared")
        c_var = sem("c_var")
        c_std = sem("c_std")
        c_h_ready = sem("c_h_ready")
        c_stored = [sem(f"c_stored{i}") for i in range(2)]
        all_added = sem("all_added")
        passed = sem("passed")
        t_loaded = [sem(f"t_loaded{i}") for i in range(TRING)]
        t_step = sem("t_step")
        t_inv_ready = sem("t_inv_ready")
        t_agg = sem("t_agg")
        t_xb = sem("t_xb")
        t_x2 = sem("t_x2")
        t_turned = sem("t_turned")
        t_copied = sem("t_copied")
        t_centered = sem("t_centered")
        t_split = sem("t_split")
        t_var = sem("t_var")
        t_std = sem("t_std")
        t_out = sem("t_out")
        t_stored = [sem(f"t_stored{i}") for i in range(TRING)]

        block = ctx.enter_context(nc.Block())

        def hold(eng):
            eng.sem_inc(passed, 1)

        def wide(ap, n):
            return ap.unsqueeze(2).broadcast_to([ap.shape[0], ap.shape[1], n])

        def rows(ap, k):
            return ap.unsqueeze(1).broadcast_to([ap.shape[0], k, ap.shape[1]])

        def group(ap, g):
            return ap[:, bass.ds(U * g, U)]

        C_AT = GROUPS
        assert CHUNKS == GROUPS

        @block.sync
        def _(sp):
            def by_edge(a):
                return a[0:P * FULL].rearrange("(p t) -> p t", p=P)

            def rest(a):
                return a[P * FULL:E].rearrange("(p t) -> p t", t=1)

            sp.wait_ge(pads_set, 3)
            for n, a in enumerate((src, dst)):
                sp.dma_start(order[:, n * TILES:n * TILES + FULL], by_edge(a)).then_inc(order_loaded, 16)
                sp.dma_start(order[0:REM, n * TILES + FULL:(n + 1) * TILES], rest(a)).then_inc(order_loaded, 16)
            sp.dma_start(type_rows[:, :], node_type.rearrange("(p c) -> p c", p=TYPE_P)).then_inc(types_loaded, 16)
            for n, a in enumerate((dst, src)):
                sp.dma_start(keys_i[:, n, 0:FULL], by_edge(a)).then_inc(keys_loaded, 16)
                sp.dma_start(keys_i[0:REM, n, FULL:TILES], rest(a)).then_inc(keys_loaded, 16)
            sp.dma_start(ew[:, 0:FULL], by_edge(edge_weight)).then_inc(ew_loaded, 16)
            sp.dma_start(ew[0:REM, FULL:TILES], rest(edge_weight)).then_inc(ew_loaded, 16)
            for t, a in ((vec_in, node_vec), (type_in, node_type)):
                sp.dma_start(t[:, 0:FULL_CHUNKS, :], a[0:FULL_CHUNKS * CHUNK].rearrange("(c p r) -> p c r", p=P, r=NR))\
                    .then_inc(nodes_loaded, 16)
                sp.dma_start(t[0:LAST_P, FULL_CHUNKS, :], a[FULL_CHUNKS * CHUNK:N].rearrange("(p r) -> p r", r=NR))\
                    .then_inc(nodes_loaded, 16)

            def load_x(t):
                sp.dma_start(x_in[0:parts(t.number), t.slot].rearrange("p r f -> p (r f)"), chunk(x, t.number))\
                    .then_inc(x_loaded[t.slot], 16)

            def store_rows(t):
                sp.wait_ge(rows_built, t.number + 1)
                sp.dma_start(chunk(table, t.number), rows_out[0:parts(t.number), t.slot].rearrange("p r f -> p (r f)"))\
                    .then_inc(rows_stored[t.slot], 16)

            for n in range(RING - 1):
                load_x(Turn(n, RING))
            for a, w in ((w1_in, W1), (w2_in, W2), (emb_in, emb), (adapt_in, adaptW)):
                sp.dma_start(a[:, :], w[:, :]).then_inc(weights_loaded, 16)
            sp.dma_start(w1T[R:R + 1, :], b1.rearrange("(a h) -> a h", a=1)).then_inc(weights_loaded, 16)
            sp.dma_start(w2T[H:H + 1, :], b2.rearrange("(a h) -> a h", a=1)).then_inc(weights_loaded, 16)
            sp.dma_start(gamma_b[:, :], gamma.rearrange("(a h) -> a h", a=1).broadcast_to([P, H])).then_inc(weights_loaded, 16)
            sp.dma_start(beta_b[:, :], beta.rearrange("(a h) -> a h", a=1).broadcast_to([P, H])).then_inc(weights_loaded, 16)

            def table_turn(t):
                a = t.ahead(RING - 1)
                if known(a, 0, CHUNKS):
                    if not a.slot_is_new:
                        sp.wait_ge(rows_built, t.number)
                    load_x(a)
                store_rows(t)
                sp.dma_start(chunk(sums, t.number), zeros[0:parts(t.number), :]).then_inc(sums_zeroed, 16)

            sp.wait_ge(const_set, 4)
            turns(sp, CHUNKS, RING, table_turn, lead=5, tail=4)

            sp.dma_start(table[N:ROWS].rearrange("(p r) f -> p (r f)", p=P), zeros[:, 0:U * W]).then_inc(trash_zeroed, 16)
            sp.dma_start(sums[N:ROWS].rearrange("(p r) f -> p (r f)", p=P), zeros[:, 0:U * W]).then_inc(sums_zeroed, 16)

            def load_attr(t):
                g = t.number
                if not t.slot_is_new:
                    sp.wait_ge(attr_turned, g - (RING - 1))
                if isinstance(g, int) and g == GROUPS - 1:
                    sp.dma_start(attr_in[:, t.slot, 0:U - 1, :],
                                 edge_attr[0:P * FULL].rearrange("(p t) r -> p t r", p=P)[:, U * g:U * g + U - 1, :])\
                        .then_inc(attr_loaded[t.slot], 16)
                    sp.dma_start(attr_in[0:REM, t.slot, U - 1, :], edge_attr[P * FULL:E]).then_inc(attr_loaded[t.slot], 16)
                else:
                    sp.dma_start(attr_in[:, t.slot, :, :],
                                 edge_attr[0:P * FULL].rearrange("(p t) r -> p t r", p=P)[:, bass.ds(U * g, U), :])\
                        .then_inc(attr_loaded[t.slot], 16)

            turns(sp, GROUPS, RING, load_attr, lead=4, tail=1)

            for i in range(RING):
                n = (CHUNKS - i + RING - 1) // RING
                sp.wait_ge(rows_stored[i], 16 * n)
            sp.wait_ge(drained, GROUPS)

            def load_c(t):
                n = parts(t.number)
                if not t.half_is_new:
                    sp.wait_ge(c_turned, 2 * (t.number - 1))
                sp.dma_start(c_x[0:n, t.half].rearrange("p r f -> p (r f)"), chunk(table, t.number))\
                    .then_inc(c_loaded[t.half], 16)

            def store_c(t):
                n = parts(t.number)
                sp.wait_ge(c_h_ready, 2 * (t.number + 1))
                sp.dma_start(chunk(hs, t.number), c_h[0:n, t.half].rearrange("p r f -> p (r f)"))\
                    .then_inc(c_stored[t.half], 16)

            def load_rows(t):
                sp.dma_start(t_x[0:parts(t.number), t.slot].rearrange("p r f -> p (r f)"), chunk(table, t.number))\
                    .then_inc(t_loaded[t.slot], 16)

            def load_h(t):
                sp.dma_start(t_h[0:parts(t.number), t.slot].rearrange("p r h -> p (r h)"), chunk(hs, t.number))\
                    .then_inc(t_loaded[t.slot], 16)

            load_c(Turn(0, RING))
            H_TURNS = 3
            H_EACH = EARLY[1] // H_TURNS
            assert H_EACH * H_TURNS == EARLY[1] and EARLY[1] * NR <= U * (GROUPS - H_TURNS)

            def turn_c(t):
                if t.k is None and 1 <= t.base <= EARLY[0]:
                    load_rows(Turn(t.base - 1, TRING))
                at = t.base - (CHUNKS + 1 - H_TURNS)
                if t.k is None and at >= 0:
                    if at == 0:
                        for i in range(2):
                            sp.wait_ge(c_stored[i], 16 * EARLY[1])
                    for n in range(at * H_EACH, (at + 1) * H_EACH):
                        load_h(Turn(n, TRING))
                if known(t, 0, CHUNKS - 1):
                    load_c(t.ahead(1))
                if known(t, 1, CHUNKS + 1):
                    store_c(t.ahead(-1))

            turns(sp, CHUNKS + 1, RING, turn_c, lead=11, tail=3)
            for i in range(2):
                sp.wait_ge(c_stored[i], 16 * ((CHUNKS - i + 1) // 2))

            def load_sums(t):
                sp.dma_start(t_s[0:parts(t.number), t.slot].rearrange("p r f -> p (r f)"), chunk(sums, t.number))\
                    .then_inc(t_loaded[t.slot], 16)

            def store_chunk(t):
                n = parts(t.number)
                sp.wait_ge(t_out, t.number + 1)
                sp.dma_start(chunk(out, t.number), t_h[0:n, t.slot].rearrange("p r f -> p (r f)"))\
                    .then_inc(t_stored[t.slot], 16)

            sp.wait_ge(all_added, 1)

            def last_turn(t):
                if known(t, TRING, CHUNKS):
                    sp.wait_ge(t_stored[t.slot], 16 * t.uses)
                if known(t, 0, CHUNKS):
                    load_sums(t)
                if known(t, EARLY[0], CHUNKS):
                    load_rows(t)
                if known(t, EARLY[1], CHUNKS):
                    load_h(t)
                if known(t, LAG, CHUNKS + LAG):
                    store_chunk(t.ahead(-LAG))

            turns(sp, CHUNKS + LAG, TRING, last_turn, lead=9, tail=11)
            for n in range(CHUNKS - TRING, CHUNKS):
                t = Turn(n, TRING)
                sp.wait_ge(t_stored[t.slot], 16 * (t.uses + 1))

        @block.gpsimd
        def _(gp):
            gp.memset(order[:, TILES - 1:TILES], 0).then_inc(pads_set, 1)
            for n in range(2):
                last = gp.iota(keys_i[:, n, FULL:TILES], pattern=[[0, 1]], base=TRASH + (U - 1) * P, channel_multiplier=1)
            gp.iota(order[:, 2 * TILES - 1:2 * TILES], pattern=[[0, 1]], base=TRASH + (U - 1) * P,
                    channel_multiplier=1).then_inc(pads_set, 1)
            gp.iota(trash_i[:, :], pattern=[[P, U]], base=TRASH, channel_multiplier=1).then_inc(const_set, 1)
            gp.iota(kind_row[:, :], pattern=[[1, LOOK]], base=0, channel_multiplier=0,
                    allow_small_or_imprecise_dtypes=True).then_inc(const_set, 1)
            gp.iota(kind_col[:, :], pattern=[[0, 1]], base=0, channel_multiplier=-1,
                    allow_small_or_imprecise_dtypes=True).then_inc(const_set, 1)
            gp.memset(zeros[:, :], 0.0).then_inc(const_set, 1)
            gp.memset(ident[:, :], 0.0).then_inc(const_set, 1)
            gp.memset(upto[:, :], 1.0).then_inc(const_set, 1)
            gp.wait_ge(const_set, 6)
            gp.affine_select(out=ident[:, :], in_=ident[:, :], compare_op=ALU.not_equal, fill=1.0, base=0,
                             pattern=[[-1, P]], channel_multiplier=1).then_inc(const_set, 1)
            for n, (m, step) in enumerate(((center[:, 0], H), (center_w[:, :], W))):
                same_row = m.rearrange("q (b h) -> q b h", b=2)
                gp.memset(m, -1.0 / H).then_inc(center_set, 1)
                gp.wait_ge(center_set, 4 * n + 1)
                gp.affine_select(out=same_row, in_=same_row, compare_op=ALU.is_ge, fill=0.0, base=0,
                                 pattern=[[-step, 2], [0, H]], channel_multiplier=1).then_inc(center_set, 1)
                gp.wait_ge(center_set, 4 * n + 2)
                gp.affine_select(out=same_row, in_=same_row, compare_op=ALU.is_ge, fill=0.0, base=H - 1,
                                 pattern=[[step, 2], [0, H]], channel_multiplier=-1).then_inc(center_set, 1)
                gp.wait_ge(center_set, 4 * n + 3)
                gp.affine_select(out=same_row, in_=same_row, compare_op=ALU.not_equal, fill=1.0 - 1.0 / H, base=0,
                                 pattern=[[-step, 2], [-1, H]], channel_multiplier=1).then_inc(center_set, 1)
            gp.affine_select(out=upto[:, 0:P], in_=upto[:, 0:P], compare_op=ALU.is_ge, fill=0.0, base=0,
                             pattern=[[1, P]], channel_multiplier=-1).then_inc(const_set, 1)

            def gather(t, source, dest):
                gp.wait_ge(idx_ready, t.number + 1)
                hold(gp)
                for u in range(U):
                    gp.indirect_dma_start(out=dest[:, t.slot, u], out_offset=None, in_=source,
                                          in_offset=bass.IndirectOffsetOnAxis(ap=slot_idx[:, t.slot, u:u + 1], axis=0))\
                        .then_inc(gathered[t.slot], 16)

            def add(t, dest):
                gp.wait_ge(put_idx_ready, t.number + 1)
                gp.wait_ge(put_ready, t.number + 1)
                hold(gp)
                for u in range(U):
                    gp.indirect_dma_start(out=dest, out_offset=bass.IndirectOffsetOnAxis(ap=put_idx[:, t.half, u:u + 1], axis=0),
                                          in_=put[:, t.half, u, :], in_offset=None, compute_op=ALU.add)\
                        .then_inc(added[t.half], 16)

            def landed(t):
                n = t.base // 2 + 1 if t.k is None else t.base // 2 + 1 + RING // 2 * t.k
                gp.wait_ge(added[t.half], 16 * U * n)
                gp.sem_inc(drained, 1)

            turns(gp, GROUPS, RING, lambda t: gather(t, x[:, :], got_x), lead=5)

            for i in range(RING):
                n = (CHUNKS - i + RING - 1) // RING
                gp.wait_ge(rows_stored[i], 16 * n)
            gp.wait_ge(trash_zeroed, 16)

            def turn_b(t):
                add(t, table[:, :])
                landed(t)

            turns(gp, GROUPS, RING, turn_b, lead=4, tail=1)

            for n in range(RING):
                gather(Turn(C_AT + n, RING), table[:, :], got)
            gp.wait_ge(sums_zeroed, 16 * (CHUNKS + 1))

            def turn_c(t):
                add(t.ahead(GROUPS), sums[:, :])
                if known(t, 0, GROUPS - RING):
                    gather(t.ahead(C_AT + RING), table[:, :], got)
                landed(t.ahead(GROUPS))

            turns(gp, GROUPS, RING, turn_c, lead=4, tail=5)
            gp.sem_inc(all_added, 1)

            def last_turn(t):
                if known(t, 0, CHUNKS):
                    n = parts(t.number)
                    gp.wait_ge(t_inv_ready, t.number + 1)
                    gp.tensor_tensor(t_s[0:n, t.slot, :, 0:H], t_s[0:n, t.slot, :, 0:H], wide(t_inv[0:n, t.slot], H), ALU.mult)\
                        .then_inc(t_agg, 1)
                if known(t, 1, CHUNKS + 1):
                    a = t.ahead(-1)
                    n = parts(a.number)
                    gp.tensor_tensor(t_x[0:n, a.slot, :, 0:H], t_x[0:n, a.slot, :, 0:H], rows(beta_b[0:n], NR), ALU.add)\
                        .then_inc(t_xb, 1)

            turns(gp, CHUNKS + 1, TRING, last_turn, lead=9, tail=5)

        @block.vector
        def _(dve):
            v = nc.vector
            st = Steps(dve, setup_step, 0)
            v.memset(attr_in[:, :, :, :], 0.0)
            st.add(v.memset(ew[:, FULL:TILES], 0.0))
            st.wait()
            dve.sem_inc(pads_set, 1)
            v.memset(half_pi[:, :], 3.141592653589793 / 2)
            v.memset(eps[:, :], EPS)
            v.memset(msg[:, :, :], 0.0)
            v.memset(attrT[:, :], 1.0)
            st.add(v.memset(hidden[:, :], 1.0))
            dve.wait_ge(order_loaded, 16 * 4)
            for n in range(RING):
                v.tensor_copy(slot_idx[:, n, :], order[:, U * n:U * (n + 1)]).then_inc(idx_ready, 1)
            def floor_of(st, out_, in_, by):
                if st.n:
                    st.wait()
                st.add(v.tensor_scalar(out_, in_, 1.0 / by, -(by - 1) / (2.0 * by), ALU.mult, ALU.add))
                st.wait()
                st.add(v.tensor_scalar(out_, out_, ROUND, None, ALU.add))
                st.wait()
                st.add(v.tensor_scalar(out_, out_, -ROUND, None, ALU.add))
                st.wait()

            st.add(v.tensor_scalar(src_col[:, :], order[:, 0:TILES], 0.0, None, ALU.add))
            floor_of(st, src_part[:, :], src_col[:, :], TYPE_COLS)
            st.add(v.scalar_tensor_tensor(out=src_col[:, :], in0=src_part[:, :], scalar=-float(TYPE_COLS), in1=src_col[:, :],
                                          op0=ALU.mult, op1=ALU.add))
            floor_of(st, src_digit[:, :], src_col[:, :], LOOK)
            st.add(v.scalar_tensor_tensor(out=src_col[:, :], in0=src_digit[:, :], scalar=-float(LOOK), in1=src_col[:, :],
                                          op0=ALU.mult, op1=ALU.add))
            dve.wait_ge(const_set, 8)
            v.tensor_scalar(ident16[:, 0], ident[:, :], float(BASE), None, ALU.mult)
            st.add(v.tensor_scalar(ident16[:, 1], ident[:, :], 1.0, None, ALU.mult))

            def take_types(t, values, g):
                if known(t, 1, 2 * GROUPS):
                    dve.wait_ge(types_turned, t.number)
                v.tensor_scalar(type4[:, :], group(values, g), 0.0, None, ALU.add).then_inc(type4_ready, 1)

            take_types(Turn(0, RING), src_part, 0)
            dve.wait_ge(types_loaded, 16)
            v.memset(type_table[:, PACK - 1, LOOK - 1:LOOK], 0.0)
            for n in range(PACK):
                wide_n = min(LOOK, TYPE_COLS - n * LOOK)
                last = v.tensor_scalar(type_table[:, n, 0:wide_n], type_rows[:, n * LOOK:n * LOOK + wide_n],
                                       float(PACK_BASE ** n), None, ALU.mult)
            last.then_inc(table_packed, 1)
            dve.wait_ge(keys_loaded, 16 * 4)
            st.add(v.tensor_copy(keys[:, :], keys_i[:, :, :].rearrange("p n t -> p (n t)")))
            st.add(v.tensor_copy(trash[:, :], trash_i[:, :]))
            st.wait()
            st.add(v.tensor_tensor(rel[:, :].rearrange("p (g u) -> p g u", u=U), keys[:, :].rearrange("p (g u) -> p g u", u=U),
                                   rows(trash[:, :], 2 * GROUPS), ALU.subtract))
            st.add(v.tensor_scalar(digit_t[:, :], keys[:, :], 1.0 / BASE, -(BASE - 1) / (2.0 * BASE), ALU.mult, ALU.add))
            st.wait()
            st.add(v.tensor_scalar(digit_t[:, :], digit_t[:, :], ROUND, None, ALU.add))
            st.wait()
            st.add(v.tensor_scalar(digit_t[:, :], digit_t[:, :], -ROUND, None, ALU.add))
            st.wait()
            v.tensor_scalar(digits[:, 0], digit_t[:, :], 0.0, None, ALU.add)
            st.add(v.scalar_tensor_tensor(out=digits[:, 1], in0=digit_t[:, :], scalar=-float(BASE), in1=keys[:, :],
                                          op0=ALU.mult, op1=ALU.add))
            dve.wait_ge(ew_loaded, 32)
            st.add(v.tensor_scalar(cw_t[:, :], ew[:, :], 0.5 / CUTOFF, ROUND, ALU.mult, ALU.add))
            st.wait()
            st.add(v.tensor_scalar(cw_t[:, :], cw_t[:, :], -ROUND, None, ALU.add))
            st.wait()
            st.add(v.scalar_tensor_tensor(out=cw_t[:, :], in0=ew[:, :], scalar=0.5 / CUTOFF, in1=cw_t[:, :],
                                          op0=ALU.mult, op1=ALU.subtract))
            st.wait()
            st.add(v.tensor_scalar(cutoff_w[:, :], cw_t[:, :], -1.0, None, ALU.mult))
            st.wait()
            v.tensor_tensor(cw_t[:, :], cw_t[:, :], cutoff_w[:, :], ALU.max).then_inc(cw_angle, 1)
            dve.wait_ge(cw_sin, 1)
            st.add(v.tensor_scalar(cw_t[:, :], cw_t[:, :], 0.5, 0.5, ALU.mult, ALU.add))
            st.add(v.tensor_scalar(cutoff_w[:, :], ew[:, :], CUTOFF, None, ALU.is_lt))
            st.wait()
            st.add(v.tensor_tensor(cutoff_w[:, :], cutoff_w[:, :], cw_t[:, :], ALU.mult))
            setup = st

            def next_idx(t):
                if known(t, 0, 2 * GROUPS - RING):
                    v.tensor_scalar(slot_idx[:, t.slot, :], order[:, bass.ds(U * (t.number + RING), U)], 0.0, None, ALU.add)\
                        .then_inc(idx_ready, 1)

            def arrived(t):
                dve.wait_ge(gathered[t.slot], 16 * U * (t.uses + 1))

            def take_keys(t):
                if not t.half_is_new:
                    dve.wait_ge(keys_turned, t.number - 1)
                v.tensor_scalar(key4[:, t.half, :], group(keys, t.number), 0.0, None, ALU.add)
                v.tensor_scalar(digit4[:, t.half], digits[:, :, bass.ds(U * t.number, U)], 0.0, None, ALU.add)\
                    .then_inc(key4_ready, 1)

            def compare_waits(t):
                dve.wait_ge(keys_turned, t.number + 1)
                dve.wait_ge(key4_ready, t.number + 1)
                if not t.half_is_new:
                    dve.wait_ge(summed, t.number - 1)

            def compare_one(t, j, last):
                made = v.scalar_tensor_tensor(out=same[:, t.half, SPAN_AT[j]:SPAN_AT[j] + SPAN[j]],
                                              in0=ps_key[:, j * P:U * P], scalar=key4[:, t.half, j:j + 1],
                                              in1=upto[:, 0:SPAN[j]], op0=ALU.is_equal, op1=ALU.mult,
                                              accum_out=count[:, t.half, j:j + 1])
                if last:
                    made.then_inc(same_ready, 1)

            def compare(t):
                compare_waits(t)
                for j in range(U):
                    compare_one(t, j, last=j == U - 1)

            def rows_to_add_to(t, st):
                dve.wait_ge(same_ready, t.number + 1)
                st.add(v.scalar_tensor_tensor(out=off4[:, :], in0=count[:, t.half], scalar=1.0, in1=group(rel, t.number),
                                              op0=ALU.is_equal, op1=ALU.mult))
                if not t.half_is_new:
                    dve.wait_ge(drained, t.number - 1)
                st.wait()
                v.tensor_tensor(put_idx[:, t.half], off4[:, :], trash[:, :], ALU.add).then_inc(put_idx_ready, 1)

            def split(t, st):
                if not t.half_is_new:
                    dve.wait_ge(summed, t.number - 1)
                m = msg_parts[:, t.half]
                st.wait()
                st.add(v.tensor_copy(m[:, 0], msg[:, :, :]))
                st.wait()
                st.add(v.tensor_tensor(left[:, :, :], msg[:, :, :], m[:, 0], ALU.subtract))
                st.wait()
                st.add(v.tensor_copy(m[:, 1], left[:, :, :]))
                st.wait()
                v.tensor_tensor(m[:, 2], left[:, :, :], m[:, 1], ALU.subtract).then_inc(msg_ready, 1)

            b0 = Steps(dve, b_step, 0)

            def copy_turned():
                dve.wait_ge(w_turned, 3)
                v.tensor_copy(w1T[0:R, :], bank[4][0:R, 0:H])
                v.tensor_copy(w2T[0:H, :], bank[4][0:H, 64:64 + H])
                v.tensor_copy(embT[:, :], bank[4][0:DIM, 128:128 + KINDS]).then_inc(w_copied, 1)

            def copy_adapted():
                dve.wait_ge(w_turned, 4)
                v.tensor_copy(adapted[:, :], bank[4][0:DIM, 256:256 + KINDS]).then_inc(w_copied, 1)
                dve.wait_ge(center_set, 8)
                dve.wait_ge(weights_loaded, 16 * 8)
                v.tensor_tensor(center[:, 1].rearrange("q (b h) -> q b h", b=2), center[:, 0].rearrange("q (b h) -> q b h", b=2),
                                rows(gamma_b[0:PAIR], 2), ALU.mult).then_inc(center_set, 1)

            def split_logits():
                dve.wait_ge(w_turned, 5)
                v.tensor_copy(logit_t[:, 0], bank[6][0:KINDS, 0:KINDS]).then_inc(w_copied, 1)
                dve.wait_ge(w_copied, 3)
                setup.add(v.tensor_copy(logits[:, 0], logit_t[:, 0]))
                setup.wait()
                setup.add(v.tensor_tensor(logit_t[:, 1], logit_t[:, 0], logits[:, 0], ALU.subtract))
                setup.wait()
                setup.add(v.tensor_copy(logits[:, 1], logit_t[:, 1]))
                setup.wait()
                v.tensor_tensor(logits[:, 2], logit_t[:, 1], logits[:, 1], ALU.subtract).then_inc(logit_split, 1)

            def compare_first():
                take_keys(Turn(0, RING))
                compare(Turn(0, RING))
                rows_to_add_to(Turn(0, RING), b0)

            A_STEPS, A_LOOK = 5, 2

            def turn_a(t):
                g = t.number
                st = Steps(dve, a_step, 0 if t.k is None and g == 0 else (A_STEPS + A_LOOK) * g - A_LOOK)
                edges, looks = known(t, 0, GROUPS), known(t, 1, GROUPS + 1)
                if known(t, 0, GROUPS - 1):
                    take_types(t.ahead(1), src_part, g + 1)
                if looks:
                    column = st.add(v.tensor_scalar(col4[:, :], group(src_col, g - 1), 0.0, None, ALU.add))
                if edges:
                    xg, d = got_x[:, t.slot], dev[:, t.slot]
                    arrived(t)
                    total = st.add(v.tensor_reduce(s4[:, :], xg, AX.X, ALU.add))
                if looks:
                    dve.wait_ge(looked, g)
                    st.wait(column)
                    for u in range(U):
                        v.scalar_tensor_tensor(out=look_hit[:, u, :], in0=kind_row[:, :], scalar=col4[:, u:u + 1],
                                               in1=ps_look[u][:, 0:LOOK], op0=ALU.is_equal, op1=ALU.mult,
                                               accum_out=found4[:, u:u + 1]).then_inc(found, 1)
                if edges:
                    st.wait(total)
                    step = st.add(v.scalar_tensor_tensor(out=d, in0=wide(s4[:, :], H), scalar=-1.0 / H, in1=xg,
                                                         op0=ALU.mult, op1=ALU.add))
                if looks:
                    dve.wait_ge(found, U * g)
                    st.add(v.tensor_scalar(group(packed, g - 1), found4[:, :], 0.0, None, ALU.add))
                if edges:
                    st.wait(step)
                    step = st.add(v.tensor_tensor(sq4[:, :, :], d, d, ALU.mult))
                    v.tensor_scalar(group(dev0, g), d, 0.0, None, ALU.max)
                    st.wait(step)
                    st.add(v.tensor_reduce(v4[:, :], sq4[:, :, :], AX.X, ALU.add))
                    next_idx(t)
                    st.wait()
                    st.add(v.tensor_scalar(group(var0, g), v4[:, :], 1.0 / H, None, ALU.mult))
                if t.k is None and g == 1:
                    copy_turned()
                if t.k is None and g == 2:
                    copy_adapted()
                if t.k is None and g == 3:
                    split_logits()
                if t.k is None and g == 4:
                    compare_first()
                if t.k is None and g == GROUPS - 1:
                    st.wait()
                    v.sem_inc(var0_ready, 1)
                assert st.n == (A_STEPS if known(t, 0, GROUPS) else 0) + (A_LOOK if looks else 0)

            turns(dve, GROUPS + 1, RING, turn_a, lead=5, tail=5)
            dve.wait_ge(a_step, (A_STEPS + A_LOOK) * GROUPS)

            dve.wait_ge(sd0_ready, 1)
            b0.add(v.reciprocal(rw[:, :], var0[:, :]))
            b0.wait()
            b0.add(v.tensor_tensor(rw[:, :], rw[:, :], ew[:, :], ALU.mult))
            b0.wait()

            B_FIRST = b0.n
            B_STEPS = 5

            def turn_b(t):
                g = t.number
                st = Steps(dve, b_step, B_FIRST + B_STEPS * g)
                edges = known(t, 0, GROUPS)
                if edges:
                    take_keys(t.ahead(1))
                    if known(t, 1, GROUPS):
                        dve.wait_ge(msg_ready, g)
                    st.add(v.tensor_tensor(msg[:, :, 0:H], group(dev0, g), wide(group(rw, g), H), ALU.mult))
                    split(t, st)
                if known(t, 1, GROUPS + 1):
                    dve.wait_ge(sig_ready, g)
                    v.tensor_tensor(hidden[0:H, :], ps_hid[0:H, :], sig[:, :], ALU.mult).then_inc(hidden_ready, 1)
                if edges:
                    compare(t.ahead(1))
                    rows_to_add_to(t.ahead(1), st)
                assert not edges or st.n == B_STEPS

            turns(dve, GROUPS + 1, RING, turn_b, lead=5, tail=1)
            dve.wait_ge(b_step, B_FIRST + B_STEPS * GROUPS)
            dve.wait_ge(gate_copied, GROUPS)

            st = Steps(dve, unpack_step, 0)
            rest_of = packed[:, :]
            for n in range(PACK - 1, 0, -1):
                floor_of(st, digit_of[:, n], rest_of, PACK_BASE ** n)
                st.add(v.scalar_tensor_tensor(out=digit_of[:, 0], in0=digit_of[:, n], scalar=-float(PACK_BASE ** n), in1=rest_of,
                                              op0=ALU.mult, op1=ALU.add))
                rest_of = digit_of[:, 0]
            for n in range(PACK):
                st.wait()
                st.add(v.scalar_tensor_tensor(out=digit_of[:, n], in0=src_digit[:, :], scalar=float(n), in1=digit_of[:, n],
                                              op0=ALU.is_equal, op1=ALU.mult))
            st.wait()
            st.add(v.tensor_tensor(type_src[:, :], digit_of[:, 0], digit_of[:, 1], ALU.add))
            st.wait()
            st.add(v.tensor_tensor(type_src[:, :], type_src[:, :], digit_of[:, 2], ALU.add))
            st.wait()

            def node_var(t):
                n = parts(t.number)
                dve.wait_ge(c_squared, 2 * t.number + 2)
                if known(t, 1, CHUNKS):
                    dve.wait_ge(c_std, t.number)
                v.tensor_reduce(c_v[0:n, :], c_q[0:n], AX.X, ALU.add).then_inc(c_var, 1)

            def node_inverse(t, st):
                n = parts(t.number)
                dve.wait_ge(c_std, t.number + 1)
                return st.add(v.reciprocal(c_r[0:n, :], c_sd[0:n, :]))

            def node_h(t, st, inverse):
                n = parts(t.number)
                if known(t, 2, CHUNKS):
                    uses = t.base // 2 if t.k is None else t.base // 2 + RING // 2 * t.k
                    dve.wait_ge(c_stored[t.half], 16 * uses)
                st.wait(inverse)
                for i in range(2):
                    v.scalar_tensor_tensor(out=c_h[0:n, t.half, i * HALF:(i + 1) * HALF],
                                           in0=ps_dev[i][0:n, 0:HALF * H].rearrange("p (r h) -> p r h", h=H), scalar=0.0,
                                           in1=wide(c_r[0:n, i * HALF:(i + 1) * HALF], H), op0=ALU.max, op1=ALU.mult)\
                        .then_inc(c_h_ready, 1)

            take_types(Turn(C_AT, RING), type_src, 0)
            take_keys(Turn(GROUPS + 1, RING))
            take_types(Turn(C_AT + 1, RING), type_src, 1)
            C_EDGE = 7

            def turn_c(t):
                g = t.number
                if t.k is None:
                    first = C_EDGE * min(g, GROUPS) + min(g, GROUPS - 1) + max(g - 1, 0)
                else:
                    first = (C_EDGE + 2) * g - 1
                st = Steps(dve, c_step, first)
                m, n = t.ahead(C_AT), t.ahead(GROUPS)
                edges, nodes = known(t, 0, GROUPS), known(t, 1, CHUNKS + 1)
                more = known(t, 0, GROUPS - 1)
                rowsg, d = got[:, m.slot], dev[:, m.slot]
                if edges:
                    arrived(m)
                    total = st.add(v.tensor_reduce(s4[:, :], rowsg[:, :, 0:H], AX.X, ALU.add))
                    st.add(v.tensor_tensor(cm4[:, :], group(cutoff_w, g), rowsg[:, :, H], ALU.mult))
                    if known(t, 1, GROUPS):
                        dve.wait_ge(msg_ready, n.number)
                    st.add(v.tensor_scalar(msg[:, :, H], rowsg[:, :, H], 0.0, None, ALU.add))
                    st.wait(total)
                    v.scalar_tensor_tensor(out=d, in0=wide(s4[:, :], H), scalar=-1.0 / H, in1=rowsg[:, :, 0:H],
                                           op0=ALU.mult, op1=ALU.add).then_inc(dev_ready, 1)
                if nodes:
                    node_var(t.ahead(-1))
                if edges:
                    dve.wait_ge(logit_done, g + 1)
                    for u in range(U):
                        if u == U // 2 and nodes:
                            inverse = node_inverse(t.ahead(-1), st)
                        last = v.scalar_tensor_tensor(out=hit[:, u, :], in0=kind_row[:, 0:KINDS], scalar=rowsg[:, u, H + 1:H + 2],
                                                      in1=ps_logit[:, u * KINDS:(u + 1) * KINDS], op0=ALU.is_equal,
                                                      op1=ALU.mult, accum_out=lg4[:, u:u + 1])
                    last.then_inc(logit_read, 1)
                elif nodes:
                    inverse = node_inverse(t.ahead(-1), st)
                if nodes:
                    node_h(t.ahead(-1), st, inverse)
                if edges:
                    dve.wait_ge(sq_ready, g + 1)
                    v.tensor_reduce(v4[:, :], sq4[:, :, :], AX.X, ALU.add).then_inc(var_ready, 1)
                    if more:
                        compare_waits(n.ahead(1))

                    def meanwhile(j, last=False):
                        if more:
                            compare_one(n.ahead(1), j, last)

                    dve.wait_ge(logit_read, g + 1)
                    st.add(v.tensor_tensor(gl4[:, :, :], group(gate, g), wide(lg4[:, :], H), ALU.add))
                    meanwhile(0)
                    dve.wait_ge(sd_ready, g + 1)
                    st.add(v.reciprocal(cf4[:, :], sd4[:, m.slot]))
                    next_idx(m)
                    st.wait()
                    st.add(v.tensor_tensor(cf4[:, :], cf4[:, :], cm4[:, :], ALU.mult))
                    st.wait()
                    st.add(v.scalar_tensor_tensor(out=d, in0=d, scalar=0.0, in1=wide(cf4[:, :], H), op0=ALU.max, op1=ALU.mult))
                    meanwhile(3)
                    st.wait()
                    v.tensor_tensor(msg[:, :, 0:H], gl4[:, :, :], d, ALU.mult).then_inc(msg_made, 1)
                    meanwhile(1)
                    dve.wait_ge(hi_made, g + 1)
                    parts_of = msg_parts[:, n.half]
                    v.tensor_tensor(left[:, :, :], msg[:, :, :], parts_of[:, 0], ALU.subtract).then_inc(left_made, 1)
                    meanwhile(2, last=True)
                    dve.wait_ge(mid_made, g + 1)
                    dve.wait_ge(left_made, g + 1)
                    v.tensor_tensor(parts_of[:, 2], left[:, :, :], parts_of[:, 1], ALU.subtract).then_inc(msg_ready, 1)
                if more:
                    rows_to_add_to(n.ahead(1), st)
                assert not edges or st.n == C_EDGE + more + (1 if nodes else 0), st.n

            turns(dve, GROUPS + 1, RING, turn_c, lead=5, tail=5)

            def clipped_tot(t, st):
                n = parts(t.number)
                dve.wait_ge(t_loaded[t.slot], 48 * (t.uses + 1))
                return st.add(v.tensor_scalar(t_inv[0:n, t.slot], t_s[0:n, t.slot, :, H], 1e-8, None, ALU.max))

            def inverse_tot(t, st, clipped):
                n = parts(t.number)
                st.wait(clipped)
                v.reciprocal(t_inv[0:n, t.slot], t_inv[0:n, t.slot]).then_inc(t_inv_ready, 1)

            def last_turn(t):
                if t.k is None:
                    first = min(t.number, CHUNKS - 1) + 2 * min(max(t.number - 4, 0), CHUNKS) + 1
                else:
                    first = 3 * t.number - 7
                st = Steps(dve, t_step, first)
                a, b = t.ahead(-3), t.ahead(-4)
                results, more = known(b, 0, CHUNKS), known(t, 0, CHUNKS - 1)
                if results:
                    n = parts(b.number)
                    y = t_s[0:n, b.slot, :, 0:H]
                    dve.wait_ge(t_std, b.number + 1)
                    inverse = st.add(v.reciprocal(t_sd[0:n, b.slot], t_sd[0:n, b.slot]))
                if more:
                    clipped = clipped_tot(t.ahead(1), st)
                if known(a, 0, CHUNKS):
                    c = parts(a.number)
                    dve.wait_ge(t_split, 2 * a.number + 2)
                    v.tensor_reduce(t_v[0:c, a.slot], t_h[0:c, a.slot], AX.X, ALU.add).then_inc(t_var, 1)
                if more:
                    inverse_tot(t.ahead(1), st, clipped)
                if results:
                    st.wait(inverse)
                    scaled = st.add(v.tensor_tensor(y, y, wide(t_sd[0:n, b.slot], H), ALU.mult))
                if known(t, 0, CHUNKS):
                    c = parts(t.number)
                    dve.wait_ge(t_agg, t.number + 1)
                    v.tensor_tensor(t_h[0:c, t.slot], t_h[0:c, t.slot], t_s[0:c, t.slot, :, 0:H], ALU.add).then_inc(t_x2, 1)
                if results:
                    st.wait(scaled)
                    dve.wait_ge(t_xb, b.number + 1)
                    v.tensor_tensor(t_h[0:n, b.slot], y, t_x[0:n, b.slot, :, 0:H], ALU.add).then_inc(t_out, 1)

            st = Steps(dve, t_step, 0)
            inverse_tot(Turn(0, TRING), st, clipped_tot(Turn(0, TRING), st))
            turns(dve, CHUNKS + 4, TRING, last_turn, lead=9, tail=8)

        @block.scalar
        def _(act):
            s = nc.scalar
            act.wait_ge(cw_angle, 1)
            s.activation(cw_t[:, :], cw_t[:, :], ACT.Sin, bias=half_pi[:, 0:1], scale=-2 * 3.141592653589793)\
                .then_inc(cw_sin, 1)
            act.wait_ge(nodes_loaded, 64)

            def one_hot(t, part, reader):
                act.wait_ge(types_turned, t.number + 1)
                if known(t, 1, 2 * GROUPS):
                    act.wait_ge(onehot_ready, t.number)
                s.activation(off_row[0:part, :], ps_type[0:part, :], ACT.Abs, bias=kind_col[0:part, 0:1]).then_inc(type_read, 1)
                act.wait_ge(type_read, t.number + 1)
                if reader is not None:
                    act.wait_ge(*reader)
                s.activation(onehot[0:part, :], off_row[0:part, :], ACT.Relu, bias=1.0, scale=-1.0).then_inc(onehot_ready, 1)

            def turn_a(t):
                n = parts(t.number)
                act.wait_ge(x_loaded[t.slot], 16 * (t.uses + 1))
                if not t.slot_is_new:
                    act.wait_ge(rows_stored[t.slot], 16 * t.uses)
                hold(act)
                at = bass.ds(t.number, 1)
                s.copy(rows_out[0:n, t.slot, :, 0:H], x_in[0:n, t.slot])
                s.copy(rows_out[0:n, t.slot, :, H], vec_in[0:n, at, :].rearrange("p a r -> p (a r)"))
                s.copy(rows_out[0:n, t.slot, :, H + 1], type_in[0:n, at, :].rearrange("p a r -> p (a r)")).then_inc(rows_built, 1)
                one_hot(t, TYPE_P, (looked, t.number) if known(t, 1, GROUPS) else None)

            turns(act, CHUNKS, RING, turn_a, lead=4, tail=1)
            act.wait_ge(var0_ready, 1)
            act.wait_ge(setup_step, 2)
            s.activation(var0[:, :], var0[:, :], ACT.Sqrt, bias=eps[:, 0:1]).then_inc(sd0_ready, 1)

            def copy_sums(t):
                act.wait_ge(summed, t.number + 1)
                if not t.half_is_new:
                    act.wait_ge(drained, t.number - 1)
                s.copy(put[:, t.half].rearrange("p u w -> p (u w)"), ps_sum[:, 0:U * W]).then_inc(put_ready, 1)

            def turn_b(t):
                g = t.number
                if known(t, 0, GROUPS):
                    act.wait_ge(attr_turned, g + 1)
                    if known(t, 1, GROUPS):
                        act.wait_ge(hid_done, g)
                    s.copy(attrT[0:R, :], ps_attr[0:R, :]).then_inc(attrT_ready, 1)
                    copy_sums(t)
                if known(t, 1, GROUPS + 1):
                    act.wait_ge(gate_done, g)
                    hold(act)
                    s.copy(group(gate, g - 1), ps_gate[:, 0:U * H].rearrange("p (u h) -> p u h", u=U)).then_inc(gate_copied, 1)
                if known(t, 0, GROUPS):
                    act.wait_ge(hid_done, g + 1)
                    if known(t, 1, GROUPS):
                        act.wait_ge(hidden_ready, g)
                    s.activation(sig[:, :], ps_hid[0:H, :], ACT.Sigmoid).then_inc(sig_ready, 1)

            turns(act, GROUPS + 1, RING, turn_b, lead=5, tail=1)

            act.wait_ge(cw_sin, 1)
            s.activation(half_pi[:, :], half_pi[:, :], ACT.Sqrt)

            def take_ahead(t):
                g = t.number
                n = t.ahead(GROUPS + 2)
                act.wait_ge(keys_turned, GROUPS + g + 1)
                act.wait_ge(same_ready, GROUPS + g + 1)
                act.wait_ge(types_turned, C_AT + g + 2)
                hold(act)
                s.copy(type4[:, :], group(type_src, g + 2)).then_inc(type4_ready, 1)
                s.copy(key4[:, n.half, :], keys[:, bass.ds(U * n.number, U)])
                s.copy(digit4[:, n.half], digits[:, :, bass.ds(U * n.number, U)]).then_inc(key4_ready, 1)

            one_hot(Turn(C_AT, RING), KINDS, (looked, GROUPS))

            def turn_c(t):
                g = t.number
                m = t.ahead(C_AT)
                edges, nodes = known(t, 0, GROUPS), known(t, 1, CHUNKS + 1)
                if edges:
                    act.wait_ge(dev_ready, g + 1)
                    s.activation(sq4[:, :, :], dev[:, m.slot], ACT.Square).then_inc(sq_ready, 1)
                if nodes:
                    n = parts(t.ahead(-1).number)
                    act.wait_ge(c_var, g)
                    if known(t, 2, CHUNKS + 1):
                        act.wait_ge(c_h_ready, 2 * (g - 1))
                    s.activation(c_sd[0:n, :], c_v[0:n, :], ACT.Sqrt, bias=eps[0:n, 0:1], scale=1.0 / H).then_inc(c_std, 1)
                if edges:
                    for i in range(2):
                        act.wait_ge(c_turned, 2 * g + i + 1)
                        if known(t, 1, CHUNKS):
                            act.wait_ge(c_centered, 2 * (g - 1) + i + 1)
                        s.copy(xT[:, i, :], ps_turn[i][0:W + H, :]).then_inc(c_copied, 1)
                    act.wait_ge(var_ready, g + 1)
                    s.activation(sd4[:, m.slot], v4[:, :], ACT.Sqrt, bias=eps[:, 0:1], scale=1.0 / H).then_inc(sd_ready, 1)
                    if known(t, 0, GROUPS - 1):
                        one_hot(m.ahead(1), KINDS, (logit_done, g + 1))
                    n = parts(g)
                    for i in range(2):
                        act.wait_ge(c_centered, 2 * g + i + 1)
                        if i == 0 and known(t, 1, CHUNKS):
                            act.wait_ge(c_var, g)
                        s.activation(c_q[0:n, i * HALF:(i + 1) * HALF].rearrange("p r h -> p (r h)"),
                                     ps_dev[i][0:n, 0:HALF * H], ACT.Square).then_inc(c_squared, 1)
                    upper_middle = msg_parts[:, t.ahead(GROUPS).half]
                    act.wait_ge(msg_made, g + 1)
                    act.wait_ge(summed, GROUPS + g - 1)
                    s.copy(upper_middle[:, 0], msg[:, :, :]).then_inc(hi_made, 1)
                    act.wait_ge(left_made, g + 1)
                    s.copy(upper_middle[:, 1], left[:, :, :]).then_inc(mid_made, 1)
                    if known(t, 0, GROUPS - 2):
                        take_ahead(t)
                    copy_sums(t.ahead(GROUPS))

            turns(act, GROUPS + 1, RING, turn_c, lead=4, tail=6)

            def deviation(t):
                n = parts(t.number)
                act.wait_ge(t_var, t.number + 1)
                s.activation(t_sd[0:n, t.slot], t_v[0:n, t.slot], ACT.Sqrt, bias=eps[0:n, 0:1], scale=1.0 / H).then_inc(t_std, 1)

            def last_turn(t):
                a = t.ahead(-1)
                for i in range(2):
                    if known(a, 0, CHUNKS):
                        n = parts(a.number)
                        act.wait_ge(t_centered, 2 * a.number + i + 1)
                        both = t_dev[(2 * a.base + i) % 3][0:n]
                        s.activation(t_h[0:n, a.slot, i * HALF:(i + 1) * HALF].rearrange("p (b i k) h -> p b i (k h)", b=2, i=2),
                                     both[:, :, :, 0, :], ACT.Square)
                        for b in range(2):
                            last = s.copy(t_s[0:n, a.slot, i * HALF + 4 * b:i * HALF + 4 * b + 4, 0:H]
                                          .rearrange("p (i k) h -> p i k h", i=2),
                                          both[:, b, :, 1, :].rearrange("p i (k h) -> p i k h", k=2))
                        last.then_inc(t_split, 1)
                    if i == 0 and known(t, 3, CHUNKS + 3):
                        deviation(t.ahead(-3))
                    if known(t, 0, CHUNKS):
                        act.wait_ge(t_turned, 2 * t.number + i + 1)
                        s.copy(xT[0:PAIR, i, :], t_turn[i][0:PAIR, :]).then_inc(t_copied, 1)

            turns(act, CHUNKS + 3, TRING, last_turn, lead=9, tail=7)

        @block.tensor
        def _(pe):
            te = nc.tensor

            def turn_types(t):
                pe.wait_ge(type4_ready, t.number + 1)
                if known(t, 1, 2 * GROUPS):
                    pe.wait_ge(type_read, t.number)
                hold(pe)
                for u in range(U):
                    last = te.matmul(ps_type[:, u * P:(u + 1) * P], type4[:, u:u + 1].broadcast_to([P, P]), ident16[:, 1],
                                     start=True, stop=True)
                last.then_inc(types_turned, 1)

            def turn_keys(t):
                pe.wait_ge(key4_ready, t.number + 1)
                if known(t, 1, 2 * GROUPS):
                    pe.wait_ge(same_ready, t.number)
                hold(pe)
                for u in range(U):
                    for n in range(2):
                        last = te.matmul(ps_key[:, u * P:(u + 1) * P], digit4[:, t.half, n, u:u + 1].broadcast_to([P, P]),
                                         ident16[:, n], start=(n == 0), stop=(n == 1))
                last.then_inc(keys_turned, 1)

            turn_types(Turn(0, RING))

            def turn_weights():
                pe.wait_ge(const_set, 8)
                pe.wait_ge(weights_loaded, 16 * 8)
                te.transpose(bank[4][0:R, 0:H], w1_in[:, :], ident[0:H, 0:H]).then_inc(w_turned, 1)
                te.transpose(bank[4][0:H, 64:64 + H], w2_in[:, :], ident[0:H, 0:H]).then_inc(w_turned, 1)
                te.transpose(bank[4][0:DIM, 128:128 + KINDS], emb_in[:, :], ident[0:KINDS, 0:KINDS]).then_inc(w_turned, 1)

            def adapt():
                pe.wait_ge(w_copied, 1)
                te.matmul(bank[4][0:DIM, 256:256 + KINDS], adapt_in[:, :], embT[:, :], start=True, stop=True).then_inc(w_turned, 1)

            def pair_logits():
                pe.wait_ge(w_copied, 2)
                te.matmul(bank[6][0:KINDS, 0:KINDS], adapted[:, :], embT[:, :], start=True, stop=True).then_inc(w_turned, 1)

            pe.wait_ge(table_packed, 1)

            def turn_a(t):
                if known(t, 0, GROUPS - 1):
                    turn_types(t.ahead(1))
                pe.wait_ge(onehot_ready, t.number + 1)
                for u in range(U):
                    if known(t, 1, GROUPS):
                        pe.wait_ge(found, U * (t.number - 1) + u + 1)
                    hold(pe)
                    for n in range(PACK):
                        last = te.matmul(ps_look[u][:, 0:LOOK], onehot[0:TYPE_P, u * P:(u + 1) * P], type_table[:, n],
                                         start=(n == 0), stop=(n == PACK - 1))
                last.then_inc(looked, 1)
                if t.k is None and t.base == 0:
                    turn_weights()
                if t.k is None and t.base == 1:
                    adapt()
                if t.k is None and t.base == 2:
                    pair_logits()
                if t.k is None and t.base == 3:
                    turn_keys(Turn(0, RING))

            turns(pe, GROUPS, RING, turn_a, lead=4, tail=1)
            pe.wait_ge(w_copied, 3)
            pe.wait_ge(found, U * GROUPS)

            def sum_equal(t):
                pe.wait_ge(same_ready, t.number + 1)
                pe.wait_ge(msg_ready, t.number + 1)
                if known(t, 1, 2 * GROUPS):
                    pe.wait_ge(put_ready, t.number)
                hold(pe)
                for i in range(U):
                    for j in range(i + 1):
                        at = SPAN_AT[j] + (i - j) * P
                        for n in range(3):
                            last = te.matmul(ps_sum[:, i * W:(i + 1) * W], same[:, t.half, at:at + P],
                                             msg_parts[:, t.half, n, j], start=(j == 0 and n == 0), stop=(j == i and n == 2))
                last.then_inc(summed, 1)


            def turn_b(t):
                g = t.number
                if known(t, 0, GROUPS):
                    turn_keys(t.ahead(1))
                    loads = 2 if isinstance(g, int) and g == GROUPS - 1 else 1
                    pe.wait_ge(attr_loaded[t.slot], 16 * (t.uses + loads))
                    if known(t, 1, GROUPS):
                        pe.wait_ge(attrT_ready, g)
                    hold(pe)
                    for u in range(U):
                        last = te.transpose(ps_attr[0:R, u * P:(u + 1) * P], attr_in[:, t.slot, u, :], ident[:, :])
                    last.then_inc(attr_turned, 1)
                    sum_equal(t)
                if known(t, 1, GROUPS + 1):
                    pe.wait_ge(hidden_ready, g)
                    if known(t, 2, GROUPS + 1):
                        pe.wait_ge(gate_copied, g - 1)
                    hold(pe)
                    for u in range(U):
                        last = te.matmul(ps_gate[:, u * H:(u + 1) * H], hidden[0:H + 1, u * P:(u + 1) * P], w2T[:, :],
                                         start=True, stop=True)
                    last.then_inc(gate_done, 1)
                if known(t, 0, GROUPS):
                    pe.wait_ge(attrT_ready, g + 1)
                    hold(pe)
                    te.matmul(ps_hid[0:H, :], w1T[:, :], attrT[0:R + 1, :], start=True, stop=True).then_inc(hid_done, 1)

            turns(pe, GROUPS + 1, RING, turn_b, lead=5, tail=5)

            def edge_logits(t):
                pe.wait_ge(onehot_ready, C_AT + t.number + 1)
                if known(t, 1, GROUPS):
                    pe.wait_ge(logit_read, t.number)
                hold(pe)
                for u in range(U):
                    for n in range(3):
                        last = te.matmul(ps_logit[:, u * KINDS:(u + 1) * KINDS], onehot[0:KINDS, u * P:(u + 1) * P], logits[:, n],
                                         start=(n == 0), stop=(n == 2))
                last.then_inc(logit_done, 1)

            pe.wait_ge(gate_copied, GROUPS)
            turn_types(Turn(C_AT, RING))
            edge_logits(Turn(0, RING))
            pe.wait_ge(center_set, 9)
            pe.wait_ge(logit_split, 1)

            def turn_c(t):
                g = t.number
                n = parts(g)
                more = known(t, 0, GROUPS - 1)
                if more:
                    turn_keys(t.ahead(GROUPS + 1))
                    turn_types(t.ahead(C_AT + 1))
                loads = t.base // 2 + 1 if t.k is None else t.base // 2 + 1 + RING // 2 * t.k
                pe.wait_ge(c_loaded[t.half], 16 * loads)
                for i in range(2):
                    if known(t, 1, CHUNKS):
                        pe.wait_ge(c_copied, 2 * (g - 1) + i + 1)
                    hold(pe)
                    for b in range(BLOCKS):
                        r = i * HALF + 2 * b
                        last = te.transpose(ps_turn[i][0:W + H, b * P:b * P + n],
                                            c_x[0:n, t.half].rearrange("p r w -> p (r w)")[:, r * W:r * W + W + H], ident[0:n, 0:n])
                    last.then_inc(c_turned, 1)
                for i in range(2):
                    pe.wait_ge(c_copied, 2 * g + i + 1)
                    if known(t, 1, CHUNKS):
                        pe.wait_ge(c_h_ready, 2 * (g - 1) + i + 1)
                    hold(pe)
                    for b in range(BLOCKS):
                        last = te.matmul(ps_dev[i][0:n, b * PAIR:(b + 1) * PAIR], xT[:, i, b * P:b * P + n], center_w[:, :],
                                         start=True, stop=True)
                    last.then_inc(c_centered, 1)
                if more:
                    edge_logits(t.ahead(1))
                sum_equal(t.ahead(GROUPS))

            turns(pe, GROUPS, RING, turn_c, lead=4, tail=1)
            pe.wait_ge(c_h_ready, 2 * CHUNKS)

            def last_turn(t):
                a = t.ahead(-1)
                for i in range(2):
                    if known(a, 0, CHUNKS):
                        n = parts(a.number)
                        pe.wait_ge(t_copied, 2 * a.number + i + 1)
                        if known(a, 2, CHUNKS):
                            pe.wait_ge(t_split, 2 * a.number + i - 2)
                        hold(pe)
                        both = t_dev[(2 * a.base + i) % 3]
                        for b in range(BLOCKS):
                            last = te.matmul(both[0:n, b // 2, b % 2].rearrange("p k f -> p (k f)"),
                                             xT[0:PAIR, i, b * P:b * P + n], center[:, :].rearrange("q k f -> q (k f)"),
                                             start=True, stop=True)
                        last.then_inc(t_centered, 1)
                    if known(t, 0, CHUNKS):
                        n = parts(t.number)
                        if i == 0:
                            pe.wait_ge(t_x2, t.number + 1)
                        if known(t, 1, CHUNKS):
                            pe.wait_ge(t_copied, 2 * (t.number - 1) + i + 1)
                        hold(pe)
                        for b in range(BLOCKS):
                            r = i * HALF + 2 * b
                            last = te.transpose(t_turn[i][0:PAIR, b * P:b * P + n],
                                                t_h[0:n, t.slot, r:r + 2].rearrange("p r h -> p (r h)"), ident[0:n, 0:n])
                        last.then_inc(t_turned, 1)

            turns(pe, CHUNKS + 1, TRING, last_turn, lead=9, tail=5)


_INS = ['x', 'src', 'dst', 'edge_attr_40', 'edge_weight', 'node_type_119', 'node_vec', 'L1_gnn_W1', 'L1_gnn_b1',
        'L1_gnn_W2', 'L1_gnn_b2', 'L1_gnn_emb', 'L1_gnn_adaptW', 'L1_gnn_gamma', 'L1_gnn_beta']


def kernel(**inputs):
    import numpy as _np
    import concourse.bacc as _bacc
    from concourse import mybir as _mybir
    from concourse.bass_utils import run_bass_kernel_spmd as _run

    nc = _bacc.Bacc("TRN2", target_bir_lowering=False, num_devices=1)
    arrays, args = {}, []
    for name in _INS:
        a = _np.ascontiguousarray(inputs[name])
        arrays[f"in_{name}_dram"] = a
        args.append(nc.dram_tensor(f"in_{name}_dram", a.shape, _mybir.dt.from_np(a.dtype), kind="ExternalInput").ap())
    shape = inputs['x'].shape
    args.append(nc.dram_tensor("out_0_dram", shape, _mybir.dt.from_np(_np.dtype('float32')), kind="ExternalOutput").ap())
    gnn_kernel(nc, *args)
    r = _run(nc, [arrays], core_ids=[0])
    return r.results[0]["out_0_dram"]
```
